# Optimizing a Trainium2 kernel written in Bass

```python
import numpy as np
import jax
import jax.numpy as jnp

def _softmax(x, axis=-1):
    return jax.nn.softmax(x, axis=axis)

def _gelu(x):
    return jax.nn.gelu(x, approximate=True)

def _silu(x):
    return jax.nn.silu(x)

def _sigmoid(x):
    return jax.nn.sigmoid(x)

def _layernorm(x, axis=-1, eps=1e-05):
    m = jnp.mean(x, axis=axis, keepdims=True)
    v = jnp.var(x, axis=axis, keepdims=True)
    return (x - m) / jnp.sqrt(v + eps)

def _scatter_add(tgt, idx, src, axis=0):
    return tgt.at[idx].add(src)

def _segment_sum(src, seg, n):
    return jax.ops.segment_sum(src, seg, n)
kernel_name = 'mk_flamingo_gated_d1_seqx_r8_dfeb8d'

def setup_inputs(seed: int=0):
    np.random.seed(seed)
    _w = jnp.asarray

    def _rec_inputs():
        import jax
        import jax.numpy as jnp
        _rk = jax.random.key(seed)
        x = -0.0002928 + 1 * jax.random.normal(jax.random.fold_in(_rk, 1), (32, 64, 128), jnp.float32)
        _lenS = 64 - jax.random.randint(jax.random.fold_in(_rk, 7), (32,), 0, max(1, 64 // 4) + 1, jnp.int32)
        _lenS2 = 64 - jax.random.randint(jax.random.fold_in(_rk, 8), (32,), 0, max(1, 64 // 4) + 1, jnp.int32)
        _ctx_1024P = jax.random.normal(jax.random.fold_in(_rk, 11), (32, 16, 128), jnp.float32)
        _ctx_1024c = jax.random.dirichlet(jax.random.fold_in(_rk, 511), 0.3 * jnp.ones((16,), jnp.float32), (32, 64))
        _ctx_1024t = jnp.einsum('bsk,bkd->bsd', _ctx_1024c, _ctx_1024P)
        _ctx_1024t = _ctx_1024t * jax.lax.rsqrt(jnp.mean(jnp.square(_ctx_1024t)) + 1e-12) * 0.953939
        ctx_1024 = -1.39393e-06 + 0.999914 * (_ctx_1024t + 0.3 * jax.random.normal(jax.random.fold_in(_rk, 611), (32, 64, 128), jnp.float32))
        _validS = jnp.arange(64)[None, :] < _lenS[:, None]
        _validS2 = jnp.arange(64)[None, :] < _lenS2[:, None]
        _causal = jnp.tril(jnp.ones((64, 64), dtype=bool))
        mask_BxSxS2_if1 = jnp.where(jnp.ones((32, 64, 64), dtype=bool), 1, 0).astype(jnp.int32)
        _g = jax.random.normal(jax.random.fold_in(_rk, 9001), (2, 1), jnp.float32)
        _g = jnp.sign(_g) * jnp.maximum(jnp.abs(_g), 1.0) + (_g == 0) * 1.0
        g_xattn = _g[0]
        g_ffn = _g[1]
        return (x, ctx_1024, mask_BxSxS2_if1, g_xattn, g_ffn)
    x, ctx_1024, mask_BxSxS2_if1, g_xattn, g_ffn = _rec_inputs()

    def _L0_xattn_setup():
        import jax, jax.numpy as jnp
        import numpy as np
        N_HEADS = 16
        D_MODEL = 128
        HEAD_DIM = D_MODEL // N_HEADS
        B, S = (2, 256)
        key = jax.random.key(seed)
        ks = jax.random.split(key, 10)
        scale = 1.0 / np.sqrt(D_MODEL)
        inp = {'query_tokens': jax.random.normal(ks[0], (B, S, D_MODEL), dtype=jnp.float32), 'key_or_value_tokens': jax.random.normal(ks[1], (B, S, D_MODEL), dtype=jnp.float32), 'mask': jnp.ones((B, S, S), dtype=jnp.int32), 'Wq': jax.random.normal(ks[2], (D_MODEL, D_MODEL), dtype=jnp.float32) * scale, 'bq': jnp.zeros((D_MODEL,), dtype=jnp.float32), 'Wk': jax.random.normal(ks[3], (D_MODEL, D_MODEL), dtype=jnp.float32) * scale, 'bk': jnp.zeros((D_MODEL,), dtype=jnp.float32), 'Wv': jax.random.normal(ks[4], (D_MODEL, D_MODEL), dtype=jnp.float32) * scale, 'bv': jnp.zeros((D_MODEL,), dtype=jnp.float32), 'Wo': jax.random.normal(ks[5], (D_MODEL, D_MODEL), dtype=jnp.float32) * scale, 'bo': jnp.zeros((D_MODEL,), dtype=jnp.float32)}
        return inp
    _L0_xattn_all = _L0_xattn_setup()
    _L0_xattn_in = {k: v for k, v in _L0_xattn_all.items() if k in ('Wq', 'bq', 'Wk', 'bk', 'Wv', 'bv', 'Wo', 'bo')}
    del _L0_xattn_all

    def _L0_ffn_setup():
        import jax, jax.numpy as jnp
        import numpy as np
        QK_SCALE = 10.0
        NEG_INF = -1000000000.0

        def layernorm(x, g, b, eps=1e-05):
            mu = jnp.mean(x, axis=-1, keepdims=True)
            var = jnp.var(x, axis=-1, keepdims=True)
            return (x - mu) * jax.lax.rsqrt(var + eps) * g + b

        def l2norm(x, eps=1e-12):
            return x / jnp.sqrt(jnp.sum(x * x, axis=-1, keepdims=True) + eps)
        key = jax.random.key(seed)
        ks = jax.random.split(key, 10)
        B, S, D, H, DH, E, FF = (2, 128, 128, 16, 64, 8, 512)
        sd = lambda fan: 1.0 / np.sqrt(fan)
        return {'x': jax.random.normal(ks[0], (B, S, D), jnp.float32), 'ln_g': jnp.ones((D,), jnp.float32), 'ln_b': jnp.zeros((D,), jnp.float32), 'Wq': jax.random.normal(ks[1], (D, H * DH), jnp.float32) * sd(D), 'Wk': jax.random.normal(ks[2], (D, H * DH), jnp.float32) * sd(D), 'Wv': jax.random.normal(ks[3], (D, H * DH), jnp.float32) * sd(D), 'q_scale': jnp.ones((H, 1, DH), jnp.float32), 'k_scale': jnp.ones((H, 1, DH), jnp.float32), 'Wo': jax.random.normal(ks[4], (H * DH, D), jnp.float32) * sd(H * DH), 'gate_w': jax.random.normal(ks[5], (D, E), jnp.float32) * sd(D), 'gate_b': jnp.zeros((E,), jnp.float32), 'w1': jax.random.normal(ks[6], (E, D, FF), jnp.float32) * sd(D), 'b1': jnp.zeros((E, FF), jnp.float32), 'w2': jax.random.normal(ks[7], (E, FF, D), jnp.float32) * sd(FF), 'b2': jnp.zeros((E, D), jnp.float32)}
    _L0_ffn_all = _L0_ffn_setup()
    _L0_ffn_in = {k: v for k, v in _L0_ffn_all.items() if k in ('ln_g', 'ln_b', 'Wq', 'Wk', 'Wv', 'q_scale', 'k_scale', 'Wo', 'gate_w', 'gate_b', 'w1', 'b1', 'w2', 'b2')}
    del _L0_ffn_all
    return {'x': x, 'ctx_1024': ctx_1024, 'mask_BxSxS2_if1': mask_BxSxS2_if1, 'g_xattn': g_xattn, 'g_ffn': g_ffn, 'L0_xattn_Wq': _L0_xattn_in['Wq'], 'L0_xattn_bq': _L0_xattn_in['bq'], 'L0_xattn_Wk': _L0_xattn_in['Wk'], 'L0_xattn_bk': _L0_xattn_in['bk'], 'L0_xattn_Wv': _L0_xattn_in['Wv'], 'L0_xattn_bv': _L0_xattn_in['bv'], 'L0_xattn_Wo': _L0_xattn_in['Wo'], 'L0_xattn_bo': _L0_xattn_in['bo'], 'L0_ffn_ln_g': _L0_ffn_in['ln_g'], 'L0_ffn_ln_b': _L0_ffn_in['ln_b'], 'L0_ffn_Wq': _L0_ffn_in['Wq'], 'L0_ffn_Wk': _L0_ffn_in['Wk'], 'L0_ffn_Wv': _L0_ffn_in['Wv'], 'L0_ffn_q_scale': _L0_ffn_in['q_scale'], 'L0_ffn_k_scale': _L0_ffn_in['k_scale'], 'L0_ffn_Wo': _L0_ffn_in['Wo'], 'L0_ffn_gate_w': _L0_ffn_in['gate_w'], 'L0_ffn_gate_b': _L0_ffn_in['gate_b'], 'L0_ffn_w1': _L0_ffn_in['w1'], 'L0_ffn_b1': _L0_ffn_in['b1'], 'L0_ffn_w2': _L0_ffn_in['w2'], 'L0_ffn_b2': _L0_ffn_in['b2']}

def reference(x, ctx_1024, mask_BxSxS2_if1, g_xattn, g_ffn, L0_xattn_Wq, L0_xattn_bq, L0_xattn_Wk, L0_xattn_bk, L0_xattn_Wv, L0_xattn_bv, L0_xattn_Wo, L0_xattn_bo, L0_ffn_ln_g, L0_ffn_ln_b, L0_ffn_Wq, L0_ffn_Wk, L0_ffn_Wv, L0_ffn_q_scale, L0_ffn_k_scale, L0_ffn_Wo, L0_ffn_gate_w, L0_ffn_gate_b, L0_ffn_w1, L0_ffn_b1, L0_ffn_w2, L0_ffn_b2):
    import jax
    import jax.numpy as jnp

    def _L0_xattn_ref(query_tokens, key_or_value_tokens, mask, Wq, bq, Wk, bk, Wv, bv, Wo, bo):
        import jax, jax.numpy as jnp
        import numpy as np
        N_HEADS = 16
        D_MODEL = 128
        HEAD_DIM = D_MODEL // N_HEADS
        B, S = (2, 256)
        b, s, d = query_tokens.shape
        h, dh = (N_HEADS, HEAD_DIM)

        def proj(x, W, bias):
            y = jnp.einsum('bsd,ed->bse', x, W) + bias
            return y.reshape(b, -1, h, dh).transpose(0, 2, 1, 3)
        q = proj(query_tokens, Wq, bq)
        k = proj(key_or_value_tokens, Wk, bk)
        v = proj(key_or_value_tokens, Wv, bv)
        scores = jnp.einsum('bhqd,bhkd->bhqk', q, k) / jnp.sqrt(jnp.float32(dh))
        scores = jnp.where(mask[:, None, :, :] == 0, jnp.float32(-1000000000.0), scores)
        attn = jax.nn.softmax(scores, axis=-1)
        out = jnp.einsum('bhqk,bhkd->bhqd', attn, v)
        out = out.transpose(0, 2, 1, 3).reshape(b, s, d)
        return jnp.einsum('bsd,ed->bse', out, Wo) + bo

    def _L0_ffn_ref(x, ln_g, ln_b, Wq, Wk, Wv, q_scale, k_scale, Wo, gate_w, gate_b, w1, b1, w2, b2):
        import jax, jax.numpy as jnp
        import numpy as np
        QK_SCALE = 10.0
        NEG_INF = -1000000000.0

        def layernorm(x, g, b, eps=1e-05):
            mu = jnp.mean(x, axis=-1, keepdims=True)
            var = jnp.var(x, axis=-1, keepdims=True)
            return (x - mu) * jax.lax.rsqrt(var + eps) * g + b

        def l2norm(x, eps=1e-12):
            return x / jnp.sqrt(jnp.sum(x * x, axis=-1, keepdims=True) + eps)
        B, S, D = x.shape
        H = q_scale.shape[0]
        DH = q_scale.shape[-1]
        h = layernorm(x, ln_g, ln_b)
        q = (h @ Wq).reshape(B, S, H, DH).transpose(0, 2, 1, 3)
        k = (h @ Wk).reshape(B, S, H, DH).transpose(0, 2, 1, 3)
        v = (h @ Wv).reshape(B, S, H, DH).transpose(0, 2, 1, 3)
        q = l2norm(q) * q_scale
        k = l2norm(k) * k_scale
        logits = jnp.einsum('bhid,bhjd->bhij', q, k) * QK_SCALE
        causal = jnp.tril(jnp.ones((S, S), bool))
        logits = jnp.where(causal, logits, NEG_INF)
        attn = jax.nn.softmax(logits, axis=-1)
        out = jnp.einsum('bhij,bhjd->bhid', attn, v)
        out = out.transpose(0, 2, 1, 3).reshape(B, S, H * DH) @ Wo
        h = layernorm(out, ln_g, ln_b)
        gate = jax.nn.softmax(h @ gate_w + gate_b, axis=-1)
        hid = jax.nn.gelu(jnp.einsum('bsd,edf->bsef', h, w1) + b1)
        exp_out = jnp.einsum('bsef,efd->bsed', hid, w2) + b2
        moe = jnp.einsum('bse,bsed->bsd', gate, exp_out)
        return layernorm(moe, ln_g, ln_b)
    x = x + jnp.tanh(g_xattn[0]) * _L0_xattn_ref(_layernorm(x, axis=-1), ctx_1024, mask_BxSxS2_if1, L0_xattn_Wq, L0_xattn_bq, L0_xattn_Wk, L0_xattn_bk, L0_xattn_Wv, L0_xattn_bv, L0_xattn_Wo, L0_xattn_bo)
    x = x + jnp.tanh(g_ffn[0]) * _L0_ffn_ref(_layernorm(x, axis=-1), L0_ffn_ln_g, L0_ffn_ln_b, L0_ffn_Wq, L0_ffn_Wk, L0_ffn_Wv, L0_ffn_q_scale, L0_ffn_k_scale, L0_ffn_Wo, L0_ffn_gate_w, L0_ffn_gate_b, L0_ffn_w1, L0_ffn_b1, L0_ffn_w2, L0_ffn_b2)
    return x

_drawn_inputs = setup_inputs


def setup_inputs(seed=0):
    import zlib

    import numpy as np

    out = dict(_drawn_inputs(seed))
    spreads = {'L0_xattn_bq': (0.0, 0.1),
     'L0_xattn_bk': (0.0, 0.1),
     'L0_xattn_bv': (0.0, 0.1),
     'L0_xattn_bo': (0.0, 0.1),
     'L0_ffn_ln_g': (1.0, 0.2),
     'L0_ffn_ln_b': (0.0, 0.1),
     'L0_ffn_q_scale': (1.0, 0.2),
     'L0_ffn_k_scale': (1.0, 0.2),
     'L0_ffn_gate_b': (0.0, 0.1),
     'L0_ffn_b1': (0.0, 0.1),
     'L0_ffn_b2': (0.0, 0.1)}
    factors = {}
    for name, (base, spread) in spreads.items():
        noise = np.random.default_rng([zlib.crc32(name.encode()), seed]).standard_normal(out[name].shape)
        drawn = base * np.exp(spread * noise) if base else spread * noise
        out[name] = jnp.asarray(drawn.astype(out[name].dtype))
    for name, factor in factors.items():
        out[name] = (out[name] * factor).astype(out[name].dtype)
    return out
```

```python
from contextlib import ExitStack

import concourse.bass as bass
from concourse import mybir

F32 = mybir.dt.float32
F32R = mybir.dt.float32r
I32 = mybir.dt.int32
ALU = mybir.AluOpType
ACT = mybir.ActivationFunctionType
AX_X = mybir.AxisListType.X

P = 128
S = 64
D = 128
HX = 16
HF = 16
C = 8
INNER = 1024
E = 8
FF = 512
NK = E * FF // P
GT = 512
EPS = 1e-5
NEG = -1e9

ROW_BQ, ROW_BK, ROW_BV, ROW_G, ROW_B, ROW_QS, ROW_KS, ROW_B1 = 0, 1, 2, 3, 4, 5, 13, 21
ROWS = ROW_B1 + NK

C_ID, C_CAUSAL, C_PAR, C_PAIR, C_VM, C_SEL = 0, 128, 192, 194, 202, 458
C_END = C_SEL + E * P


def gated_block(nc, consts, x, ctx_in, mask, g_xattn, g_ffn, xwq, xbq, xwk, xbk, xwv, xbv, xwo, xbo,
                ln_g, ln_b, wq, wk, wv, q_scale, k_scale, wo, gate_w, gate_b, w1, b1, w2, b2, out):
    B = x.shape[0]
    TILES = B * S // P
    GROUPS = B * S // GT
    PER = GT // P
    x_t = x.rearrange("(t b) s d -> (t b s) d", b=2)
    c_t = ctx_in.rearrange("(t b) s d -> (t b s) d", b=2)
    m_t = mask.rearrange("b q k -> q b k")
    out_t = out.rearrange("(t b) s d -> (b s) t d", b=2)

    def row(v):
        return v.rearrange("(a d) -> a d", a=1)

    def ge(eng, sem, value):
        if not isinstance(value, int) or value > 0:
            eng.wait_ge(sem, value)

    with ExitStack() as stack:
        def sb(name, shape, dt=F32):
            return stack.enter_context(nc.sbuf_tensor(name, shape, dt))

        def psum(name, shape):
            return stack.enter_context(nc.psum_tensor(name, shape, F32))

        def sem(name):
            return stack.enter_context(nc.semaphore(name))

        ps_s = psum("ps_s", [P, 2, 512])
        ps_t = psum("ps_t", [P, 2, 512])
        ps_q = psum("ps_q", [P, 2, 512])
        ps_x = psum("ps_x", [P, 512])
        ps_y = psum("ps_y", [P, 512])

        cst = sb("cst", [P, C_END])
        ident = cst[:, C_ID:C_ID + P]
        causal = cst[:, C_CAUSAL:C_CAUSAL + S]
        par_mask = cst[:, C_PAR:C_PAR + 2]
        pair_mask = cst[:, C_PAIR:C_PAIR + C]
        v_mask = cst[:, C_VM:C_VM + 2 * P].rearrange("p (h f) -> p h f", h=2)
        sel = sb("sel", [E, E * P], F32R)
        rows = sb("rows", [ROWS, P])
        cols = sb("cols", [P, ROWS])
        qk_scale = sb("qk_scale", [P, C])
        bo_b = sb("bo_b", [P, D])
        g_b = sb("g_b", [P, D])
        b_b = sb("b_b", [P, D])
        gate_bb = sb("gate_bb", [P, E])
        gates_in = sb("gates_in", [P, 2])
        tanh_g = sb("tanh_g", [P, 2])
        tg_bo = sb("tg_bo", [P, D])
        tg_g = sb("tg_g", [P, D])
        tg_b = sb("tg_b", [P, D])
        eps2 = sb("eps2", [P, 3])
        xwT = sb("xwT", [P, 4, D])
        stage = sb("stage", [P, NK * P])
        wqkv = stage[:, 0:3 * INNER].rearrange("p (a n) -> p a n", a=3)
        xw = stage[:, 3 * INNER:3 * INNER + 4 * D].rearrange("p (a d) -> p a d", a=4)
        w1_s = stage[:, :].rearrange("p (k f) -> p k f", f=P)
        wqkv_hi = sb("wqkv_hi", [P, 3, INNER], F32R)
        wqkv_lo = sb("wqkv_lo", [P, 3, INNER], F32R)
        wo_s = sb("wo_s", [P, C, D])
        gate_ws = sb("gate_ws", [P, E])
        w1_hi = sb("w1_hi", [P, NK, P], F32R)
        w1_lo = sb("w1_lo", [P, NK, P], F32R)
        w2_s = stage[:, :].rearrange("p (k d) -> p k d", d=D)
        b2_s = sb("b2_s", [E, D])
        b2_hi = sb("b2_hi", [E, D], F32R)
        b2_lo = sb("b2_lo", [E, D], F32R)

        x1_all = sb("x1_all", [P, TILES * D])
        h_hi = sb("h_hi", [P, TILES * P], F32R)
        h_lo = sb("h_lo", [P, TILES * P], F32R)
        gates = sb("gates", [P, TILES * E])
        y_stat = sb("y_stat", [P, PER, 6])
        y_mv = sb("y_mv", [P, TILES, 2])
        y_mg = sb("y_mg", [P, PER, 2])
        y_ln = sb("y_ln", [P, TILES])
        y_r = sb("y_r", [P, TILES])
        shared = nc.sbuf_base

        x_in = sb("x_in", [P, 2, D])
        c_in = sb("c_in", [P, 2, D])
        m_in = sb("m_in", [P, 2, 2, S], I32)
        x_stat = sb("x_stat", [P, 6])
        x_mv = sb("x_mv", [P, 2])
        x_ln = sb("x_ln", [P, 2])
        x_n = sb("x_n", [P, D])
        xnT = sb("xnT", [P, P])
        ctxT = sb("ctxT", [P, 2, 2, S])
        xq_m = sb("xq_m", [P, 2, 2, S])
        xk_T = sb("xk_T", [P, 2, S])
        xk_m = sb("xk_m", [P, 2, C, S])
        xv_m = sb("xv_m", [P, 2, 2, P])
        x_log = sb("x_log", [P, 2 * C, S])
        x_sh = sb("x_sh", [P, 2 * C, S])
        x_p = x_pn = x_sh
        x_mx = sb("x_mx", [P, 2 * C])
        x_sum = sb("x_sum", [P, 2 * C])
        x_rs = sb("x_rs", [P, 2 * C])
        x_pT = sb("x_pT", [P, 2, 4, 2, S])
        x_aT = sb("x_aT", [P, P])
        x_u = sb("x_u", [P, D])
        x1 = sb("x1", [P, D])

        a_stat = sb("a_stat", [P, 6])
        a_mv = sb("a_mv", [P, 2])
        a_ln = sb("a_ln", [P, 2])
        a_n = sb("a_n", [P, D])
        a_hT = sb("a_hT", [P, P])
        a_hi = sb("a_hi", [P, P], F32R)
        a_lo = sb("a_lo", [P, P], F32R)
        a_sq = sb("a_sq", [P, 2, HF, S])
        a_ss = sb("a_ss", [P, 2, HF])
        a_lnss = sb("a_lnss", [P, 2, HF])
        a_r = sb("a_r", [P, 2, HF])
        a_qk = sb("a_qk", [P, 2, HF, S])
        a_qT = sb("a_qT", [P, C, P])
        a_kT = sb("a_kT", [P, C, P])
        a_v = sb("a_v", [P, 2, INNER])
        b_log = sb("b_log", [P, 2 * C, S])
        b_sh = sb("b_sh", [P, 2 * C, S])
        b_p = b_pn = b_sh
        b_mx = sb("b_mx", [P, 2 * C])
        b_sum = sb("b_sum", [P, 2 * C])
        b_rs = sb("b_rs", [P, 2 * C])
        b_pT = sb("b_pT", [P, C, 2, S])
        b_aT = sb("b_aT", [P, C, 2, S])
        b_stat = sb("b_stat", [P, 6])
        b_mv = sb("b_mv", [P, 2])
        b_ln = sb("b_ln", [P, 2])
        b_n = sb("b_n", [P, D])
        b_hT = sb("b_hT", [P, P])
        b_gl = sb("b_gl", [P, E])
        b_gm = sb("b_gm", [P, 1])
        b_ge = sb("b_ge", [P, E])
        b_gs = sb("b_gs", [P, 1])
        b_gr = sb("b_gr", [P, 1])
        end = nc.sbuf_base

        RING = 4

        def over(name, shape, dt=F32):
            nonlocal shared
            t = nc.alloc_sbuf_tensor_at(name, shape, dt, offset=shared)
            size = 4
            for n in shape[1:]:
                size *= n
            shared += size
            assert shared <= end
            return t

        w2_hi = over("w2_hi", [P, NK, D], F32R)
        w2_lo = over("w2_lo", [P, NK, D], F32R)
        hid = over("hid", [P, RING, GT])
        hid_hi = over("hid_hi", [P, RING, GT], F32R)
        hid_lo = over("hid_lo", [P, RING, GT], F32R)
        g_cur = over("g_cur", [P, PER * E])
        gT_hi = over("gT_hi", [E, GT], F32R)
        gT_lo = over("gT_lo", [E, GT], F32R)
        gate_row = over("gate_row", [P, 2, GT])
        e_out = over("e_out", [P, 2, GT])
        y_T = over("y_T", [P, GT])
        y_all = over("y_all", [P, TILES * D])

        consts_in = sem("consts_in")
        weights_in = sem("weights_in")
        experts_in = sem("experts_in")
        inputs_in = [sem(f"inputs_in{p}") for p in range(2)]
        setup_T, setup_cols, setup_xwT, setup_tanh = sem("setup_T"), sem("setup_cols"), sem("setup_xwT"), sem("setup_tanh")
        setup_dve, setup_split, setup_bo, w1_split = sem("setup_dve"), sem("setup_split"), sem("setup_bo"), sem("w1_split")
        names = ("xst xmv xl xr xn xT xct xc xproj xqm xkT xkm xvm xlogits xneg xmask xmax xshift xexp xsum xrs xnorm "
                 "xPT xpT xpv xaT xo xu x1d x1s "
                 "ast amv al ar an aT ahT ahi alo aq ak asq ass aln arr aqn akn av avd aqT aqTd akT akTd "
                 "bs blog bmax bsh bexp bsum brs bnorm bPT bpT bpv baT bo bst bmv bl br bn bT bhT bhi blo "
                 "bg bgl bgm bge bgr bgn").split()
        s = {n: sem("s_" + n) for n in names}
        hid_ps, hid_done, hid_used = sem("hid_ps"), sem("hid_done"), sem("hid_used")
        hi_done, lo_done, w2_hi_done, w2_lo_done = sem("hi_done"), sem("lo_done"), sem("w2_hi_done"), sem("w2_lo_done")
        g_cur_done, gT_ps, gT_hi_done, gT_lo_done = sem("g_cur_done"), sem("gT_ps"), sem("gT_hi_done"), sem("gT_lo_done")
        row_ps, row_done, out_done = sem("row_ps"), sem("row_done"), sem("out_done")
        acc_done, y_ps, y_done, yT_ps = sem("acc_done"), sem("y_ps"), sem("y_done"), sem("yT_ps")
        y_stats, y_mvs, y_kept, yl, yr = sem("y_stats"), sem("y_mvs"), sem("y_kept"), sem("yl"), sem("yr")
        f1, f2, f3, stored, xb_done = sem("f1"), sem("f2"), sem("f3"), sem("stored"), sem("xb_done")

        y_ag, passed = sem("y_ag"), sem("passed")

        def hold(eng, sm, value):
            ge(eng, sm, value)
            if not isinstance(value, int):
                eng.sem_inc(passed, 1)

        def counts(eng, t):
            if isinstance(t, int):
                return t + 1, t, t - 1
            return eng.snap(t + 1), eng.snap(t + 0), eng.snap(t - 1)

        def run_tiles(eng, body):
            for t in range(3):
                body(t, t % 2, t)
            with eng.Fori(1, TILES // 2 - 1) as j:
                body(2 * j + 1, 1, None)
                body(2 * j + 2, 0, None)
            for t in range(TILES - 1, TILES + 2):
                body(t, t % 2, t)

        def has(static, stage):
            return static is None or 0 <= static - stage < TILES

        def hid_bank(k):
            return (ps_s if k % 4 < 2 else ps_t)[:, k % 2, :]

        flat = lambda ap: ap[:, :, :].rearrange("p a b -> p (a b)")
        block = stack.enter_context(nc.Block())

        @block.sync
        def _(sp):
            sp.dma_start(cst[:, 0:C_SEL], consts[:, 0:C_SEL]).then_inc(consts_in, 16)
            sp.dma_start(cst[0:E, C_SEL:C_END], consts[0:E, C_SEL:C_END]).then_inc(consts_in, 16)
            for j, w in enumerate((xwq, xwk, xwv, xwo)):
                sp.dma_start(xw[:, j, :], w).then_inc(consts_in, 16)
            for r, v in ((ROW_BQ, xbq), (ROW_BK, xbk), (ROW_BV, xbv), (ROW_G, ln_g), (ROW_B, ln_b)):
                sp.dma_start(rows[r:r + 1, :], row(v)).then_inc(consts_in, 16)
            sp.dma_start(rows[ROW_QS:ROW_QS + C, :], q_scale.rearrange("(c h) a d -> c (h a d)", h=2)).then_inc(consts_in, 16)
            sp.dma_start(rows[ROW_KS:ROW_KS + C, :], k_scale.rearrange("(c h) a d -> c (h a d)", h=2)).then_inc(consts_in, 16)
            sp.dma_start(rows[ROW_B1:ROWS, :], b1.rearrange("e (c f) -> (e c) f", f=P)).then_inc(consts_in, 16)

            def load(t, p):
                sp.dma_start(x_in[:, p, :], x_t[bass.ts(t, P)]).then_inc(inputs_in[p], 16)
                sp.dma_start(c_in[:, p, :], c_t[bass.ts(t, P)]).then_inc(inputs_in[p], 16)
                for h in range(2):
                    sp.dma_start(m_in[h * S:(h + 1) * S, p, :, :], m_t[:, bass.ts(t, 2), :]).then_inc(inputs_in[p], 16)

            load(0, 0)
            load(1, 1)
            for j, w in enumerate((wq, wk, wv)):
                sp.dma_start(wqkv[:, j, :], w).then_inc(weights_in, 16)
            sp.dma_start(wo_s[:, :, :], wo.rearrange("(c p) d -> p c d", p=P)).then_inc(weights_in, 16)
            sp.dma_start(gate_ws[:, :], gate_w).then_inc(weights_in, 16)
            sp.dma_start(b2_s[:, :], b2).then_inc(weights_in, 16)
            sp.wait_ge(setup_T, 4)
            sp.wait_ge(setup_split, 2)
            sp.dma_start(stage[:, :].rearrange("p (e f) -> p e f", e=E), w1.rearrange("e d f -> d e f")).then_inc(experts_in, 16)
            for t in range(2):
                sp.wait_ge(s["x1d"], t + 1)
                load(t + 2, t)
            sp.wait_ge(w1_split, 2)
            sp.dma_start(w2_s, w2.rearrange("e (c p) d -> p (e c) d", p=P)).then_inc(experts_in, 16)
            with sp.Fori(1, TILES // 2 - 1) as j:
                i = 2 * j
                for p in range(2):
                    sp.wait_ge(s["x1d"], i + (p + 1))
                    load(i + (p + 2), p)

        @block.gpsimd
        def _(pool):
            pool.wait_ge(weights_in, 96)
            pool.tensor_copy(wqkv_hi[:, :, :], wqkv[:, :, :]).then_inc(setup_split, 1)
            pool.wait_ge(setup_split, 1)
            pool.tensor_tensor(wqkv_lo[:, :, :], wqkv[:, :, :], wqkv_hi[:, :, :].bitcast(F32), ALU.subtract).then_inc(setup_split, 1)

            def body(t, p, static):
                X1, A1, B1 = counts(pool, t)
                if has(static, 0):
                    hold(pool, s["xshift"], A1)
                    pool.memset(flat(x_log), NEG).then_inc(s["xneg"], 1)
                if has(static, 2):
                    ge(pool, s["bmax"], B1)
                    pool.tensor_tensor(b_sh[:, :, :], b_log[:, :, :], b_mx[:, :].unsqueeze(2).to_broadcast([P, 2 * C, S]),
                                       ALU.subtract).then_inc(s["bsh"], 1)
                if has(static, 0):
                    ge(pool, s["xkT"], X1)
                    pool.tensor_tensor(xk_m[:, :, :, :], xk_T[:, :, :].unsqueeze(2).to_broadcast([P, 2, C, S]),
                                       pair_mask.unsqueeze(1).unsqueeze(3).to_broadcast([P, 2, C, S]),
                                       ALU.mult).then_inc(s["xkm"], 1)
                if has(static, 2):
                    ge(pool, s["brs"], B1)
                    pool.tensor_tensor(b_pn[:, :, :], b_p[:, :, :], b_rs[:, :].unsqueeze(2).to_broadcast([P, 2 * C, S]),
                                       ALU.mult).then_inc(s["bnorm"], 1)
                if has(static, 0):
                    ge(pool, s["xmax"], X1)
                    pool.tensor_tensor(x_sh[:, :, :], x_log[:, :, :], x_mx[:, :].unsqueeze(2).to_broadcast([P, 2 * C, S]),
                                       ALU.subtract).then_inc(s["xshift"], 1)
                    ge(pool, s["xrs"], X1)
                    pool.tensor_tensor(x_pn[:, :, :], x_p[:, :, :], x_rs[:, :].unsqueeze(2).to_broadcast([P, 2 * C, S]),
                                       ALU.mult).then_inc(s["xnorm"], 1)
                if static == 0:
                    pool.wait_ge(experts_in, 16)
                    pool.tensor_copy(w1_hi[:, :, :], w1_s).then_inc(w1_split, 1)
                if static == 1:
                    pool.wait_ge(w1_split, 1)
                    pool.tensor_tensor(w1_lo[:, :, :], w1_s,
                                       w1_hi[:, :, :].bitcast(F32), ALU.subtract).then_inc(w1_split, 1)
                    pool.tensor_copy(b2_hi[:, :], b2_s[:, :]).then_inc(w1_split, 1)
                    pool.wait_ge(w1_split, 3)
                    pool.tensor_tensor(b2_lo[:, :], b2_s[:, :], b2_hi[:, :].bitcast(F32), ALU.subtract).then_inc(w1_split, 1)

            run_tiles(pool, body)

            pool.wait_ge(s["blo"], TILES)
            pool.wait_ge(s["bgn"], TILES)
            pool.wait_ge(experts_in, 32)
            for e in range(E):
                pool.tensor_copy(w2_hi[:, 4 * e:4 * e + 4, :], w2_s[:, 4 * e:4 * e + 4, :]).then_inc(w2_hi_done, 1)

            def experts(g, first):
                for k in range(NK):
                    ge(pool, hid_done, g * NK + (k + 1))
                    if first:
                        hold(pool, hid_used, k + 1 - RING)
                    else:
                        hold(pool, hid_used, g * NK + (k + 1 - RING))
                    pool.tensor_copy(hid_hi[:, k % RING, :], hid[:, k % RING, :]).then_inc(hi_done, 1)
                    if k % 4 == 3 and k > 4:
                        add_expert(g, k // 4 - 1, first)
                add_expert(g, E - 1, first)

            def add_expert(g, e, first):
                ge(pool, out_done, g * E + (e + 1))
                if e == 0:
                    if not first:
                        hold(pool, y_kept, g)
                    ins = pool.tensor_copy(y_T[:, :], e_out[:, e % 2, :])
                else:
                    ge(pool, acc_done, g * E + e)
                    ins = pool.tensor_tensor(y_T[:, :], y_T[:, :], e_out[:, e % 2, :], ALU.add)
                ins.then_inc(acc_done, 1)

            experts(0, True)
            with pool.Fori(1, GROUPS) as g:
                experts(g, False)

        @block.scalar
        def _(act):
            for tile, v in ((bo_b, xbo), (g_b, ln_g), (b_b, ln_b), (gate_bb, gate_b)):
                act.dma_start(tile[:, :], v.partition_broadcast(P)).then_inc(setup_bo, 16)
            for j, v in enumerate((g_xattn, g_ffn)):
                act.dma_start(gates_in[:, j:j + 1], v.partition_broadcast(P)).then_inc(setup_bo, 16)
            act.wait_ge(setup_bo, 96)
            act.activation(tanh_g[:, :], gates_in[:, :], ACT.Tanh).then_inc(setup_tanh, 1)
            act.wait_ge(setup_T, 4)
            act.copy(flat(xwT), ps_s[:, 0, :]).then_inc(setup_xwT, 1)
            act.wait_ge(setup_dve, 2)

            def body(t, p, static):
                X1, A1, B1 = counts(act, t)
                if has(static, 0):
                    ge(act, s["xmv"], X1)
                    act.activation(x_ln[:, 0:1], x_mv[:, 1:2], ACT.Ln, bias=eps2[:, 0:1]).then_inc(s["xl"], 1)
                    ge(act, s["xl"], X1)
                    act.activation(x_ln[:, 1:2], x_ln[:, 0:1], ACT.Exp, scale=-0.5).then_inc(s["xr"], 1)
                if has(static, 1):
                    ge(act, s["amv"], A1)
                    act.activation(a_ln[:, 0:1], a_mv[:, 1:2], ACT.Ln, scale=1.0 + EPS, bias=eps2[:, 1:2]).then_inc(s["al"], 1)
                    ge(act, s["al"], A1)
                    act.activation(a_ln[:, 1:2], a_ln[:, 0:1], ACT.Exp, scale=-0.5).then_inc(s["ar"], 1)
                if has(static, 0):
                    ge(act, s["xT"], X1)
                    act.copy(xnT[:, :], ps_x[:, 0:P]).then_inc(s["xct"], 1)
                    act.copy(ctxT[:, :, :, :], ps_x[:, P:2 * P].rearrange("p (b k) -> p b k", b=2).unsqueeze(2)
                             .to_broadcast([P, 2, 2, S])).then_inc(s["xc"], 1)
                    ge(act, s["xproj"], X1)
                    act.activation(xk_T[:, :, :].rearrange("p b k -> p (b k)"), ps_x[:, P:2 * P], ACT.Identity,
                                   bias=cols[:, ROW_BK:ROW_BK + 1]).then_inc(s["xkT"], 1)
                if has(static, 1):
                    ge(act, s["aT"], A1)
                    act.activation(a_hT[:, :], ps_y[:, 0:P], ACT.Identity, scale=cols[:, ROW_G:ROW_G + 1],
                                   bias=cols[:, ROW_B:ROW_B + 1]).then_inc(s["ahT"], 1)
                    ge(act, s["ahT"], A1)
                    act.copy(a_hi[:, :], a_hT[:, :]).then_inc(s["ahi"], 1)
                if has(static, 2):
                    ge(act, s["bsh"], B1)
                    act.activation(flat(b_p), flat(b_sh), ACT.Exp).then_inc(s["bexp"], 1)
                if has(static, 1):
                    ge(act, s["aq"], A1)
                    act.activation(a_sq[:, 0, :, :].rearrange("p h d -> p (h d)"), ps_q[:, :, :].rearrange("p a b -> p (a b)"),
                                   ACT.Square).then_inc(s["asq"], 1)
                    ge(act, s["ak"], A1)
                    act.activation(a_sq[:, 1, :, :].rearrange("p h d -> p (h d)"), ps_t[:, :, :].rearrange("p a b -> p (a b)"),
                                   ACT.Square).then_inc(s["asq"], 1)
                    ge(act, s["ass"], A1)
                    act.activation(flat(a_lnss), flat(a_ss), ACT.Ln, bias=eps2[:, 2:3]).then_inc(s["aln"], 1)
                    ge(act, s["aln"], A1)
                    act.activation(flat(a_r), flat(a_lnss), ACT.Exp, scale=-0.5).then_inc(s["arr"], 1)
                if has(static, 2):
                    ge(act, s["bPT"], B1)
                    act.copy(b_pT[:, :, :, :].rearrange("p c h q -> p (c h q)"), flat(ps_t)).then_inc(s["bpT"], 1)
                if has(static, 1):
                    ge(act, s["av"], A1)
                    act.copy(a_v[:, 1 - p, :], flat(ps_q)).then_inc(s["avd"], 1)
                if has(static, 0):
                    ge(act, s["xshift"], X1)
                    act.activation(flat(x_p), flat(x_sh), ACT.Exp).then_inc(s["xexp"], 1)
                if has(static, 2):
                    ge(act, s["bpv"], B1)
                    act.copy(b_aT[:, :, :, :], ps_q[:, :, :].rearrange("p b (c q) -> p c b q", c=C)).then_inc(s["baT"], 1)
                if has(static, 1):
                    ge(act, s["akT"], A1)
                    act.copy(flat(a_kT), flat(ps_t)).then_inc(s["akTd"], 1)
                if has(static, 2):
                    ge(act, s["bmv"], B1)
                    act.activation(b_ln[:, 0:1], b_mv[:, 1:2], ACT.Ln, bias=eps2[:, 0:1]).then_inc(s["bl"], 1)
                    ge(act, s["bl"], B1)
                    act.activation(b_ln[:, 1:2], b_ln[:, 0:1], ACT.Exp, scale=-0.5).then_inc(s["br"], 1)
                if has(static, 0):
                    ge(act, s["xPT"], X1)
                    act.copy(x_pT[:, :, :, :, :].rearrange("p b j h q -> p (b j h q)"), flat(ps_t)).then_inc(s["xpT"], 1)
                if has(static, 2):
                    u = t - 2
                    ge(act, s["bT"], B1)
                    act.activation(b_hT[:, :], ps_y[:, 0:P], ACT.Identity, scale=cols[:, ROW_G:ROW_G + 1],
                                   bias=cols[:, ROW_B:ROW_B + 1]).then_inc(s["bhT"], 1)
                    hold(act, s["bhT"], B1)
                    act.copy(h_hi[:, bass.ts(u, P)], b_hT[:, :]).then_inc(s["bhi"], 1)
                    ge(act, s["bgm"], B1)
                    act.activation(b_ge[:, :], b_gl[:, :], ACT.Exp, bias=b_gm[:, 0:1], accum_out=b_gs[:, 0:1]).then_inc(s["bge"], 1)

            run_tiles(act, body)

            def gelu(g, k):
                ge(act, hid_ps, g * NK + (k + 1))
                if isinstance(g, int) and g == 0:
                    ge(act, lo_done, k + 1 - RING)
                else:
                    act.wait_ge(lo_done, g * NK + (k + 1 - RING))
                act.activation(hid[:, k % RING, :], hid_bank(k), ACT.Gelu_apprx_tanh,
                               bias=cols[:, ROW_B1 + k:ROW_B1 + k + 1]).then_inc(hid_done, 1)

            for k in range(NK):
                gelu(0, k)
            with act.Fori(1, GROUPS) as g:
                for k in range(NK):
                    gelu(g, k)
            act.wait_ge(y_mvs, GROUPS)
            act.activation(y_ln[:, :], y_mv[:, :, 1], ACT.Ln, bias=eps2[:, 0:1]).then_inc(yl, 1)
            act.wait_ge(yl, 1)
            act.activation(y_r[:, :], y_ln[:, :], ACT.Exp, scale=-0.5).then_inc(yr, 1)
            for c in range(GROUPS):
                act.wait_ge(f3, c + 1)
                act.dma_start(out_t[:, c * PER:(c + 1) * PER, :], y_all[:, c * PER * D:(c + 1) * PER * D]
                              .rearrange("p (t d) -> p t d", d=D)).then_inc(stored, 16)
            act.wait_ge(stored, 16 * GROUPS)

        @block.vector
        def _(dve):
            for j, e in enumerate((EPS, EPS * EPS, 1e-12)):
                dve.memset(eps2[:, j:j + 1], e).then_inc(setup_dve, 1)
            dve.wait_ge(setup_T, 5)
            dve.tensor_copy(cols[:, :], ps_x[:, 0:ROWS]).then_inc(setup_cols, 1)
            dve.wait_ge(setup_cols, 1)
            dve.scalar_tensor_tensor(qk_scale[:, :], cols[:, ROW_QS:ROW_QS + C], 10.0, cols[:, ROW_KS:ROW_KS + C],
                                     ALU.mult, ALU.mult).then_inc(setup_cols, 1)
            dve.tensor_copy(sel[:, :], cst[0:E, C_SEL:C_END]).then_inc(setup_cols, 1)
            dve.wait_ge(setup_tanh, 1)
            dve.tensor_scalar(tg_bo[:, :], bo_b[:, :], tanh_g[:, 0:1], None, ALU.mult).then_inc(setup_cols, 1)
            dve.tensor_scalar(tg_g[:, :], g_b[:, :], tanh_g[:, 1:2], None, ALU.mult).then_inc(setup_cols, 1)
            dve.tensor_scalar(tg_b[:, :], b_b[:, :], tanh_g[:, 1:2], None, ALU.mult).then_inc(setup_cols, 1)
            dve.wait_ge(setup_cols, 6)

            def body(t, p, static):
                X1, A1, B1 = counts(dve, t)
                if has(static, 0):
                    tp = t - p
                    ge(dve, inputs_in[p], (32 * tp + 64) if isinstance(t, int) else dve.snap(32 * t + (64 - 32 * p)))
                    dve.bn_stats(x_stat[:, :], x_in[:, p, :]).then_inc(s["xst"], 1)
                if has(static, 1):
                    ge(dve, s["x1d"], A1)
                    dve.bn_stats(a_stat[:, :], x1[:, :]).then_inc(s["ast"], 1)
                if has(static, 0):
                    hold(dve, s["xst"], X1)
                    dve.bn_aggr(x_mv[:, :], x_stat[:, :]).then_inc(s["xmv"], 1)
                if has(static, 1):
                    hold(dve, s["ast"], A1)
                    dve.bn_aggr(a_mv[:, :], a_stat[:, :]).then_inc(s["amv"], 1)
                if has(static, 0):
                    ge(dve, s["xr"], X1)
                    dve.tensor_scalar(x_n[:, :], x_in[:, p, :], x_mv[:, 0:1], x_ln[:, 1:2], ALU.subtract,
                                      ALU.mult).then_inc(s["xn"], 1)
                if has(static, 1):
                    ge(dve, s["ar"], A1)
                    dve.tensor_scalar(a_n[:, :], x1[:, :], a_mv[:, 0:1], a_ln[:, 1:2], ALU.subtract,
                                      ALU.mult).then_inc(s["an"], 1)
                if has(static, 2):
                    ge(dve, s["bs"], B1)
                    dve.tensor_tensor(b_log[:, :, :], ps_s[:, :, :].rearrange("p a (c k) -> p (a c) k", k=S),
                                      causal.unsqueeze(1).to_broadcast([P, 2 * C, S]), ALU.add).then_inc(s["blog"], 1)
                    ge(dve, s["blog"], B1)
                    dve.tensor_reduce(b_mx[:, :], b_log[:, :, :], AX_X, ALU.max).then_inc(s["bmax"], 1)
                if has(static, 0):
                    ge(dve, s["xkT"], X1)
                    for h in range(2):
                        dve.tensor_scalar(xq_m[:, :, h, :], ps_x[:, 0:P].rearrange("p (b q) -> p b q", b=2),
                                          cols[:, ROW_BQ:ROW_BQ + 1], par_mask[:, h:h + 1], ALU.add,
                                          ALU.mult).then_inc(s["xqm"], 1)
                    dve.tensor_tensor(xv_m[:, :, :, :], ps_x[:, 2 * P:4 * P].rearrange("p (b f) -> p b f", b=2).unsqueeze(2)
                                      .to_broadcast([P, 2, 2, P]), v_mask.unsqueeze(1).to_broadcast([P, 2, 2, P]),
                                      ALU.mult).then_inc(s["xvm"], 1)
                if has(static, 1):
                    ge(dve, s["ahi"], A1)
                    dve.tensor_tensor(a_lo[:, :], a_hT[:, :], a_hi[:, :].bitcast(F32), ALU.subtract).then_inc(s["alo"], 1)
                if has(static, 2):
                    ge(dve, s["bexp"], B1)
                    dve.tensor_reduce(b_sum[:, :], b_p[:, :, :], AX_X, ALU.add).then_inc(s["bsum"], 1)
                    ge(dve, s["bsum"], B1)
                    dve.reciprocal(b_rs[:, :], b_sum[:, :]).then_inc(s["brs"], 1)
                if has(static, 1):
                    A2 = 2 * t if isinstance(t, int) else dve.snap(2 * t)
                    ge(dve, s["asq"], A2)
                    dve.tensor_reduce(a_ss[:, :, :], a_sq[:, :, :, :], AX_X, ALU.add).then_inc(s["ass"], 1)
                    ge(dve, s["arr"], A1)
                    dve.tensor_tensor(a_qk[:, 0, :, :], ps_q[:, :, :].rearrange("p a (h d) -> p (a h) d", d=S),
                                      a_r[:, 0, :].unsqueeze(2).to_broadcast([P, HF, S]), ALU.mult).then_inc(s["aqn"], 1)
                    dve.tensor_tensor(a_qk[:, 1, :, :], ps_t[:, :, :].rearrange("p a (h d) -> p (a h) d", d=S),
                                      a_r[:, 1, :].unsqueeze(2).to_broadcast([P, HF, S]), ALU.mult).then_inc(s["akn"], 1)
                if has(static, 0):
                    ge(dve, s["xneg"], X1)
                    hold(dve, s["xlogits"], X1)
                    for b in range(2):
                        dve.copy_predicated(x_log[:, b * C:(b + 1) * C, :], m_in[:, p, b, :].unsqueeze(1).to_broadcast([P, C, S]),
                                            ps_s[:, b, :].rearrange("p (c k) -> p c k", k=S)).then_inc(s["xmask"], 1)
                    X2 = 2 * t + 2 if isinstance(t, int) else dve.snap(2 * t + 2)
                    ge(dve, s["xmask"], X2)
                    dve.tensor_reduce(x_mx[:, :], x_log[:, :, :], AX_X, ALU.max).then_inc(s["xmax"], 1)
                if has(static, 1):
                    ge(dve, s["aqT"], A1)
                    dve.tensor_tensor(a_qT[:, :, :], ps_t[:, :, :].rearrange("p a (c q) -> p (a c) q", q=P),
                                      qk_scale[:, :].unsqueeze(2).to_broadcast([P, C, P]), ALU.mult).then_inc(s["aqTd"], 1)
                if has(static, 0):
                    ge(dve, s["xexp"], X1)
                    dve.tensor_reduce(x_sum[:, :], x_p[:, :, :], AX_X, ALU.add).then_inc(s["xsum"], 1)
                    ge(dve, s["xsum"], X1)
                    dve.reciprocal(x_rs[:, :], x_sum[:, :]).then_inc(s["xrs"], 1)
                if has(static, 2):
                    u = t - 2
                    ge(dve, s["bo"], B1)
                    dve.bn_stats(b_stat[:, :], ps_y[:, 0:D]).then_inc(s["bst"], 1)
                    hold(dve, s["bst"], B1)
                    dve.bn_aggr(b_mv[:, :], b_stat[:, :]).then_inc(s["bmv"], 1)
                    ge(dve, s["br"], B1)
                    dve.tensor_scalar(b_n[:, :], ps_y[:, 0:D], b_mv[:, 0:1], b_ln[:, 1:2], ALU.subtract,
                                      ALU.mult).then_inc(s["bn"], 1)
                    ge(dve, s["bhi"], B1)
                    dve.tensor_tensor(h_lo[:, bass.ts(u, P)], b_hT[:, :], h_hi[:, bass.ts(u, P)].bitcast(F32),
                                      ALU.subtract).then_inc(s["blo"], 1)
                    ge(dve, s["bg"], B1)
                    dve.tensor_tensor(b_gl[:, :], ps_y[:, 0:E], gate_bb[:, :], ALU.add).then_inc(s["bgl"], 1)
                    ge(dve, s["bgl"], B1)
                    dve.tensor_reduce(b_gm[:, :], b_gl[:, :], AX_X, ALU.max, negate=True).then_inc(s["bgm"], 1)
                    ge(dve, s["bge"], B1)
                    dve.reciprocal(b_gr[:, :], b_gs[:, :]).then_inc(s["bgr"], 1)
                    ge(dve, s["bgr"], B1)
                    dve.tensor_scalar(gates[:, bass.ts(u, E)], b_ge[:, :], b_gr[:, 0:1], None, ALU.mult).then_inc(s["bgn"], 1)
                if has(static, 0):
                    ge(dve, s["xpv"], X1)
                    dve.tensor_scalar(x_aT[:, :], ps_x[:, 0:P], cols[:, ROW_BV:ROW_BV + 1], None, ALU.add).then_inc(s["xaT"], 1)
                    ge(dve, s["xo"], X1)
                    dve.scalar_tensor_tensor(x_u[:, :], ps_x[:, P:2 * P], tanh_g[:, 0:1], tg_bo[:, :], ALU.mult,
                                             ALU.add).then_inc(s["xu"], 1)
                    ge(dve, s["xu"], X1)
                    dve.tensor_tensor(x1[:, :], x_u[:, :], x_in[:, p, :], ALU.add).then_inc(s["x1s"], 1)
                    dve.tensor_tensor(x1_all[:, bass.ts(t, D)], x_u[:, :], x_in[:, p, :], ALU.add).then_inc(s["x1d"], 1)

            run_tiles(dve, body)

            dve.wait_ge(w2_hi_done, E)
            for e in range(E):
                dve.tensor_tensor(w2_lo[:, 4 * e:4 * e + 4, :], w2_s[:, 4 * e:4 * e + 4, :],
                                  w2_hi[:, 4 * e:4 * e + 4, :].bitcast(F32), ALU.subtract).then_inc(w2_lo_done, 1)

            def weigh(g, e, first):
                ge(dve, hid_used, g * NK + (4 * e + 4))
                ge(dve, row_done, g * E + (e + 1))
                if first:
                    ge(dve, acc_done, e - 1)
                else:
                    dve.wait_ge(acc_done, g * E + (e - 1))
                dve.tensor_tensor(e_out[:, e % 2, :], ps_q[:, e % 2, :], gate_row[:, e % 2, :], ALU.mult).then_inc(out_done, 1)

            def experts(g, first):
                if not first:
                    dve.wait_ge(gT_ps, g)
                dve.tensor_copy(g_cur[:, :], gates[:, bass.ts(g, PER * E)]).then_inc(g_cur_done, 1)
                for k in range(NK):
                    if k == 0:
                        ge(dve, gT_ps, g + 1)
                        dve.tensor_copy(gT_hi[:, :], ps_y[0:E, :]).then_inc(gT_hi_done, 1)
                        ge(dve, gT_hi_done, g + 1)
                        dve.tensor_tensor(gT_lo[:, :], ps_y[0:E, :], gT_hi[:, :].bitcast(F32), ALU.subtract).then_inc(gT_lo_done, 1)
                    ge(dve, hi_done, g * NK + (k + 1))
                    dve.tensor_tensor(hid_lo[:, k % RING, :], hid[:, k % RING, :], hid_hi[:, k % RING, :].bitcast(F32),
                                      ALU.subtract).then_inc(lo_done, 1)
                    if k % 4 == 2:
                        e = k // 4
                        ge(dve, row_ps, g * E + (e + 1))
                        dve.tensor_copy(gate_row[:, e % 2, :], ps_x[:, :]).then_inc(row_done, 1)
                    if k % 4 == 3 and k > 4:
                        weigh(g, k // 4 - 1, first)
                weigh(g, E - 1, first)
                ge(dve, acc_done, g * E + E)
                ge(dve, y_ps, g + 1)
                dve.tensor_tensor(y_T[:, :], ps_y[:, :], y_T[:, :], ALU.add).then_inc(y_done, 1)
                ge(dve, yT_ps, g + 1)
                for c in range(PER):
                    dve.bn_stats(y_stat[:, c, :], ps_y[:, c * P:(c + 1) * P]).then_inc(y_stats, 1)
                dve.tensor_copy(y_all[:, bass.ts(g, PER * D)], ps_y[:, :]).then_inc(y_kept, 1)
                hold(dve, y_stats, g * PER + PER)
                for c in range(PER):
                    ins = dve.bn_aggr(y_mg[:, c, :], y_stat[:, c, :]).then_inc(y_ag, 1)
                ge(dve, y_ag, g * PER + PER)
                dve.tensor_copy(flat(y_mv)[:, bass.ts(g, PER * 2)], flat(y_mg)).then_inc(y_mvs, 1)

            experts(0, True)
            with dve.Fori(1, GROUPS) as g:
                experts(g, False)
            dve.wait_ge(yr, 1)
            for c in range(TILES):
                yc = y_all[:, c * D:(c + 1) * D]
                dve.tensor_scalar(yc, yc, y_mv[:, c, 0:1], y_r[:, c:c + 1], ALU.subtract, ALU.mult).then_inc(f1, 1)
            for g in range(GROUPS):
                w = slice(g * PER * D, (g + 1) * PER * D)
                y3 = y_all[:, w].rearrange("p (t d) -> p t d", d=D)
                x3 = x1_all[:, w].rearrange("p (t d) -> p t d", d=D)
                dve.wait_ge(f1, TILES)
                dve.tensor_tensor(y3, y3, tg_g[:, :].unsqueeze(1).to_broadcast([P, PER, D]), ALU.mult).then_inc(f2, 1)
                dve.tensor_tensor(x3, x3, tg_b[:, :].unsqueeze(1).to_broadcast([P, PER, D]), ALU.add).then_inc(f2, 1)
                dve.wait_ge(f2, 2 * g + 2)
                dve.tensor_tensor(y3, y3, x3, ALU.add).then_inc(f3, 1)

        @block.tensor
        def _(pe):
            pe.wait_ge(consts_in, 16 * 14)
            for j in range(4):
                pe.transpose(ps_s[:, 0, j * P:(j + 1) * P], xw[:, j, :], ident).then_inc(setup_T, 1)
            pe.transpose(ps_x[:, 0:ROWS], rows[:, :], cst[0:ROWS, C_ID:C_ID + ROWS]).then_inc(setup_T, 1)
            pe.wait_ge(setup_xwT, 1)
            pe.wait_ge(setup_cols, 3)

            def split_mm(o, l_hi, l_lo, r_hi, r_lo, start=True, stop=True):
                pe.matmul(o, l_hi, r_hi, start=start, stop=False)
                pe.matmul(o, l_hi, r_lo, start=False, stop=False)
                return pe.matmul(o, l_lo, r_hi, start=False, stop=stop)

            def body(t, p, static):
                X1, A1, B1 = counts(pe, t)
                if has(static, 0):
                    ge(pe, s["xn"], X1)
                    ge(pe, s["xvm"], A1)
                    pe.transpose(ps_x[:, 0:P], x_n[:, :], ident)
                    pe.transpose(ps_x[:, P:2 * P], c_in[:, p, :], ident).then_inc(s["xT"], 1)
                if has(static, 2):
                    hold(pe, s["akTd"], B1)
                    hold(pe, s["aqTd"], B1)
                    hold(pe, s["xmask"], 2 * min(t, TILES) if isinstance(t, int) else pe.snap(2 * t))
                    for c in range(C):
                        for b in range(2):
                            for h in range(2):
                                o = ps_s[h * S:(h + 1) * S, c // 4, (c % 4) * P + b * S:(c % 4) * P + (b + 1) * S]
                                last = pe.matmul(o, a_qT[h * S:(h + 1) * S, c, b * S:(b + 1) * S],
                                                 a_kT[h * S:(h + 1) * S, c, b * S:(b + 1) * S], start=True, stop=True)
                    last.then_inc(s["bs"], 1)
                if has(static, 0):
                    ge(pe, s["xc"], X1)
                    pe.matmul(ps_x[:, 0:P], xwT[:, 0, :], xnT[:, :], start=True, stop=True)
                    pe.matmul(ps_x[:, P:2 * P], xwT[:, 1, :], ctxT[:, :, 0, :], start=True, stop=True)
                    for b in range(2):
                        last = pe.matmul(ps_x[:, (2 + b) * P:(3 + b) * P], ctxT[:, b, :, :].rearrange("p a k -> p (a k)"),
                                         xwT[:, 2, :], start=True, stop=True)
                    last.then_inc(s["xproj"], 1)
                if has(static, 1):
                    ge(pe, s["an"], A1)
                    ge(pe, s["bgl"], B1 - 1 if isinstance(B1, int) else pe.snap(t - 2))
                    pe.transpose(ps_y[:, 0:P], a_n[:, :], ident).then_inc(s["aT"], 1)
                    if isinstance(static, int) and static == 1:
                        pe.wait_ge(setup_split, 2)
                    ge(pe, s["alo"], A1)
                    ge(pe, s["baT"], B1 - 1 if isinstance(B1, int) else pe.snap(t - 2))
                    for n in range(2):
                        w = slice(n * 512, (n + 1) * 512)
                        last = split_mm(ps_q[:, n, :], a_hi[:, :], a_lo[:, :], wqkv_hi[:, 0, w], wqkv_lo[:, 0, w])
                    last.then_inc(s["aq"], 1)
                    ge(pe, s["xpT"], A1)
                    for n in range(2):
                        w = slice(n * 512, (n + 1) * 512)
                        last = split_mm(ps_t[:, n, :], a_hi[:, :], a_lo[:, :], wqkv_hi[:, 1, w], wqkv_lo[:, 1, w])
                    last.then_inc(s["ak"], 1)
                if has(static, 2):
                    ge(pe, s["bnorm"], B1)
                    ge(pe, s["akn"], min(t, TILES) if isinstance(t, int) else A1)
                    for c in range(C):
                        last = pe.transpose(ps_t[:, c // 4, (c % 4) * P:(c % 4 + 1) * P],
                                            b_pn[:, 2 * c:2 * c + 2, :].rearrange("p b k -> p (b k)"), ident)
                    last.then_inc(s["bPT"], 1)
                if has(static, 0):
                    ge(pe, s["blog"], B1)
                    ge(pe, s["xkm"], X1)
                    ge(pe, s["xqm"], 2 * t + 2 if isinstance(t, int) else pe.snap(2 * t + 2))
                    for b in range(2):
                        last = pe.matmul(ps_s[:, b, :], xq_m[:, b, :, :].rearrange("p h q -> p (h q)"),
                                         xk_m[:, b, :, :].rearrange("p c k -> p (c k)"), start=True, stop=True)
                    last.then_inc(s["xlogits"], 1)
                if has(static, 1):
                    ge(pe, s["aqn"], A1)
                    for n in range(2):
                        w = slice(n * 512, (n + 1) * 512)
                        last = split_mm(ps_q[:, n, :], a_hi[:, :], a_lo[:, :], wqkv_hi[:, 2, w], wqkv_lo[:, 2, w])
                    last.then_inc(s["av"], 1)
                    ge(pe, s["akn"], A1)
                    ge(pe, s["bpT"], B1)
                    for c in range(C):
                        last = pe.transpose(ps_t[:, c // 4, (c % 4) * P:(c % 4 + 1) * P],
                                            a_qk[:, 0, 2 * c:2 * c + 2, :].rearrange("p h d -> p (h d)"), ident)
                    last.then_inc(s["aqT"], 1)
                if has(static, 2):
                    hold(pe, s["bpT"], B1)
                    hold(pe, s["avd"], min(t, TILES) if isinstance(t, int) else A1)
                    for c in range(C):
                        for h in range(2):
                            for b in range(2):
                                last = pe.matmul(ps_q[h * S:(h + 1) * S, b, c * S:(c + 1) * S],
                                                 a_v[b * S:(b + 1) * S, p, (2 * c + h) * S:(2 * c + h + 1) * S],
                                                 b_pT[b * S:(b + 1) * S, c, h, :], start=True, stop=True)
                    last.then_inc(s["bpv"], 1)
                if has(static, 1):
                    ge(pe, s["aqTd"], A1)
                    for c in range(C):
                        last = pe.transpose(ps_t[:, c // 4, (c % 4) * P:(c % 4 + 1) * P],
                                            a_qk[:, 1, 2 * c:2 * c + 2, :].rearrange("p h d -> p (h d)"), ident)
                    last.then_inc(s["akT"], 1)
                if has(static, 2):
                    ge(pe, s["baT"], B1)
                    ge(pe, s["ahT"], min(t, TILES) if isinstance(t, int) else A1)
                    for c in range(C):
                        last = pe.matmul(ps_y[:, 0:D], b_aT[:, c, :, :].rearrange("p b q -> p (b q)"), wo_s[:, c, :],
                                         start=(c == 0), stop=(c == C - 1))
                    last.then_inc(s["bo"], 1)
                if has(static, 0):
                    ge(pe, s["xnorm"], X1)
                    ge(pe, s["akTd"], A1)
                    for b in range(2):
                        for j in range(4):
                            last = pe.transpose(ps_t[:, b, j * P:(j + 1) * P],
                                                x_pn[:, b * C + 2 * j:b * C + 2 * j + 2, :].rearrange("p c k -> p (c k)"), ident)
                    last.then_inc(s["xPT"], 1)
                if has(static, 2):
                    ge(pe, s["bn"], B1)
                    pe.transpose(ps_y[:, 0:P], b_n[:, :], ident).then_inc(s["bT"], 1)
                if has(static, 0):
                    ge(pe, s["xkT"], X1)
                    ge(pe, s["xvm"], X1)
                    ge(pe, s["xpT"], X1)
                    for b in range(2):
                        for j in range(4):
                            for h in range(2):
                                last = pe.matmul(ps_x[32 * j:32 * (j + 1), b * S:(b + 1) * S],
                                                 xv_m[:, b, h, 32 * j:32 * (j + 1)], x_pT[:, b, j, h, :],
                                                 start=(h == 0), stop=(h == 1))
                    last.then_inc(s["xpv"], 1)
                if has(static, 2):
                    ge(pe, s["bhT"], B1)
                    pe.matmul(ps_y[:, 0:E], b_hT[:, :], gate_ws[:, :], start=True, stop=True).then_inc(s["bg"], 1)
                if has(static, 0):
                    ge(pe, s["xaT"], X1)
                    pe.matmul(ps_x[:, P:2 * P], x_aT[:, :], xwT[:, 3, :], start=True, stop=True).then_inc(s["xo"], 1)

            run_tiles(pe, body)

            LAG = 3

            def experts(g, first):
                tok = bass.ts(g, GT)
                for k in range(NK + LAG):
                    if k < NK:
                        if first:
                            ge(pe, hid_done, k + 1 - RING)
                        else:
                            pe.wait_ge(hid_done, g * NK + (k + 1 - RING))
                        split_mm(hid_bank(k), w1_hi[:, k, :], w1_lo[:, k, :], h_hi[:, tok], h_lo[:, tok]).then_inc(hid_ps, 1)
                    if k == 0:
                        ge(pe, g_cur_done, g + 1)
                        if not first:
                            pe.wait_ge(y_kept, g)
                        for c in range(PER):
                            last = pe.transpose(ps_y[0:E, c * P:(c + 1) * P], g_cur[:, c * E:(c + 1) * E], ident)
                        last.then_inc(gT_ps, 1)
                    if k % 4 == 2 and k < NK:
                        e = k // 4
                        ge(pe, gT_lo_done, g + 1)
                        if first:
                            ge(pe, row_done, e)
                        else:
                            pe.wait_ge(row_done, g * E + e)
                        pe.matmul(ps_x[:, :], sel[:, e * P:(e + 1) * P], gT_hi[:, :], start=True, stop=False)
                        pe.matmul(ps_x[:, :], sel[:, e * P:(e + 1) * P], gT_lo[:, :], start=False, stop=True).then_inc(row_ps, 1)
                    if k >= LAG:
                        j = k - LAG
                        e = j // 4
                        if j % 4 == 0:
                            if first:
                                ge(pe, out_done, e - 1)
                                pe.wait_ge(w2_lo_done, e + 1)
                            else:
                                pe.wait_ge(out_done, g * E + (e - 1))
                        ge(pe, lo_done, g * NK + (j + 1))
                        mm = split_mm(ps_q[:, e % 2, :], w2_hi[:, j, :], w2_lo[:, j, :], hid_hi[:, j % RING, :],
                                      hid_lo[:, j % RING, :], start=(j % 4 == 0), stop=(j % 4 == 3))
                        mm.then_inc(hid_used, 1)
                split_mm(ps_y[:, :], b2_hi[:, :], b2_lo[:, :], gT_hi[:, :], gT_lo[:, :]).then_inc(y_ps, 1)
                ge(pe, y_done, g + 1)
                for c in range(PER):
                    last = pe.transpose(ps_y[:, c * P:(c + 1) * P], y_T[:, c * P:(c + 1) * P], ident)
                last.then_inc(yT_ps, 1)

            pe.wait_ge(w1_split, 4)
            pe.wait_ge(s["blo"], TILES)
            pe.wait_ge(s["xpT"], TILES)
            experts(0, True)
            with pe.Fori(1, GROUPS) as g:
                experts(g, False)


_INS = ['x', 'ctx_1024', 'mask_BxSxS2_if1', 'g_xattn', 'g_ffn', 'L0_xattn_Wq', 'L0_xattn_bq', 'L0_xattn_Wk', 'L0_xattn_bk',
        'L0_xattn_Wv', 'L0_xattn_bv', 'L0_xattn_Wo', 'L0_xattn_bo', 'L0_ffn_ln_g', 'L0_ffn_ln_b', 'L0_ffn_Wq', 'L0_ffn_Wk',
        'L0_ffn_Wv', 'L0_ffn_q_scale', 'L0_ffn_k_scale', 'L0_ffn_Wo', 'L0_ffn_gate_w', 'L0_ffn_gate_b', 'L0_ffn_w1',
        'L0_ffn_b1', 'L0_ffn_w2', 'L0_ffn_b2']


def _constants(np):
    t = np.zeros((P, C_END), np.float32)
    i = np.arange(P)
    t[i, C_ID + i] = 1.0
    t[:, C_CAUSAL:C_CAUSAL + S] = np.where(np.arange(S)[None, :] <= (i % S)[:, None], 0.0, NEG)
    head = i // (D // HX)
    for h in range(2):
        t[:, C_PAR + h] = (head % 2 == h) / np.sqrt(np.float32(D // HX))
        t[:, C_VM + h * P:C_VM + (h + 1) * P] = (head % 2 == h)[None, :] & ((head // 2 % 2)[None, :] == (i // S)[:, None])
    for c in range(C):
        t[:, C_PAIR + c] = head // 2 == c
    for e in range(E):
        t[e, C_SEL + e * P:C_SEL + (e + 1) * P] = 1.0
    return t


def kernel(**inputs):
    import numpy as _np
    import concourse.bacc as _bacc
    from concourse import mybir as _mybir
    from concourse.bass_utils import run_bass_kernel_spmd as _run

    nc = _bacc.Bacc("TRN2", target_bir_lowering=False, num_devices=1)
    arrays = {"in_constants_dram": _constants(_np)}
    args = [nc.dram_tensor("in_constants_dram", (P, C_END), _mybir.dt.float32, kind="ExternalInput").ap()]
    for name in _INS:
        a = _np.ascontiguousarray(inputs[name])
        arrays[f"in_{name}_dram"] = a
        args.append(nc.dram_tensor(f"in_{name}_dram", a.shape, _mybir.dt.from_np(a.dtype), kind="ExternalInput").ap())
    out = nc.dram_tensor("out_0_dram", inputs["x"].shape, _mybir.dt.float32, kind="ExternalOutput").ap()
    gated_block(nc, *args, out)
    r = _run(nc, [arrays], core_ids=[0])
    return r.results[0]["out_0_dram"]
```

```python
from contextlib import ExitStack

import concourse.bass as bass
from concourse import mybir

F32 = mybir.dt.float32
F32R = mybir.dt.float32r
I32 = mybir.dt.int32
ALU = mybir.AluOpType
ACT = mybir.ActivationFunctionType
AX_X = mybir.AxisListType.X

P = 128
S = 64
D = 128
HX = 16
HF = 16
C = 8
INNER = 1024
E = 8
FF = 512
NK = E * FF // P
GT = 512
EPS = 1e-5
NEG = -1e9
NEVER = -2.0 ** 30

ROW_BQ, ROW_BK, ROW_BV, ROW_G, ROW_B, ROW_QS, ROW_KS, ROW_B1 = 0, 1, 2, 3, 4, 5, 13, 21
ROWS = ROW_B1 + NK

C_ID, C_CAUSAL, C_PAR, C_PAIR, C_VM, C_SEL = 0, 128, 192, 194, 202, 458
C_END = C_SEL + E * P


def gated_block(nc, consts, x, ctx_in, mask, g_xattn, g_ffn, xwq, xbq, xwk, xbk, xwv, xbv, xwo, xbo,
                ln_g, ln_b, wq, wk, wv, q_scale, k_scale, wo, gate_w, gate_b, w1, b1, w2, b2, out):
    B = x.shape[0]
    TILES = B * S // P
    GROUPS = B * S // GT
    PER = GT // P
    x_t = x.rearrange("(t b) s d -> (t b s) d", b=2)
    c_t = ctx_in.rearrange("(t b) s d -> (t b s) d", b=2)
    m_t = mask.rearrange("b q k -> q b k")
    out_t = out.rearrange("(t b) s d -> (b s) t d", b=2)

    def row(v):
        return v.rearrange("(a d) -> a d", a=1)

    def ge(eng, sem, value):
        if not isinstance(value, int) or value > 0:
            eng.wait_ge(sem, value)

    with ExitStack() as stack:
        def sb(name, shape, dt=F32):
            return stack.enter_context(nc.sbuf_tensor(name, shape, dt))

        def psum(name, shape):
            return stack.enter_context(nc.psum_tensor(name, shape, F32))

        def sem(name):
            return stack.enter_context(nc.semaphore(name))

        ps_s = psum("ps_s", [P, 2, 512])
        ps_t = psum("ps_t", [P, 2, 512])
        ps_q = psum("ps_q", [P, 2, 512])
        ps_x = psum("ps_x", [P, 512])
        ps_y = psum("ps_y", [P, 512])

        cst = sb("cst", [P, C_END])
        ident = cst[:, C_ID:C_ID + P]
        causal = cst[:, C_CAUSAL:C_CAUSAL + S]
        par_mask = cst[:, C_PAR:C_PAR + 2]
        pair_mask = cst[:, C_PAIR:C_PAIR + C]
        v_mask = cst[:, C_VM:C_VM + 2 * P].rearrange("p (h f) -> p h f", h=2)
        sel = sb("sel", [E, E * P], F32R)
        ident_r = sb("ident_r", [P, P], F32R)
        causal_r = sb("causal_r", [P, C, S], F32R)
        bq_par = sb("bq_par", [P, 2])
        rows = sb("rows", [ROWS, P])
        cols = sb("cols", [P, ROWS])
        qk_scale = sb("qk_scale", [P, C])
        bo_b = sb("bo_b", [P, D])
        g_b = sb("g_b", [P, D])
        b_b = sb("b_b", [P, D])
        gate_bb = sb("gate_bb", [P, E])
        gates_in = sb("gates_in", [P, 2])
        tanh_g = sb("tanh_g", [P, 2])
        tg_bo = sb("tg_bo", [P, D])
        tg_g = sb("tg_g", [P, D])
        tg_b = sb("tg_b", [P, D])
        eps2 = sb("eps2", [P, 3])
        xwT = sb("xwT", [P, 4, D])
        stage = sb("stage", [P, NK * P])
        wqkv = stage[:, 0:3 * INNER].rearrange("p (a n) -> p a n", a=3)
        xw = stage[:, 3 * INNER:3 * INNER + 4 * D].rearrange("p (a d) -> p a d", a=4)
        w1_s = stage[:, :].rearrange("p (k f) -> p k f", f=P)
        wqkv_hi = sb("wqkv_hi", [P, 3, INNER], F32R)
        wqkv_lo = sb("wqkv_lo", [P, 3, INNER], F32R)
        wo_s = sb("wo_s", [P, C, D])
        gate_ws = sb("gate_ws", [P, E])
        w1_hi = sb("w1_hi", [P, NK, P], F32R)
        w1_lo = sb("w1_lo", [P, NK, P], F32R)
        w2_s = stage[:, :].rearrange("p (k d) -> p k d", d=D)
        b2_s = sb("b2_s", [E, D])
        b2_hi = sb("b2_hi", [E, D], F32R)
        b2_lo = sb("b2_lo", [E, D], F32R)

        x1_all = sb("x1_all", [P, TILES * D])
        h_hi = sb("h_hi", [P, TILES * P], F32R)
        h_lo = sb("h_lo", [P, TILES * P], F32R)
        gates = sb("gates", [P, TILES * E])
        y_stat = sb("y_stat", [P, PER, 6])
        y_mv = sb("y_mv", [P, TILES, 2])
        y_mg = sb("y_mg", [P, PER, 2])
        y_ln = sb("y_ln", [P, TILES])
        y_r = sb("y_r", [P, TILES])
        shared = nc.sbuf_base

        x_in = sb("x_in", [P, 2, D])
        c_in = sb("c_in", [P, 2, D])
        m_in = sb("m_in", [P, 2, 2, S], I32)
        x_stat = sb("x_stat", [P, 6])
        x_mv = sb("x_mv", [P, 2])
        x_ln = sb("x_ln", [P, 2])
        x_n = sb("x_n", [P, D])
        xnT = sb("xnT", [P, P])
        ctxT = sb("ctxT", [P, 2, 2, S])
        xq_m = sb("xq_m", [P, 2, 2, S])
        xk_T = sb("xk_T", [P, 2, S])
        xk_m = sb("xk_m", [P, 2, C, S])
        xv_m = sb("xv_m", [P, 2, 2, 2, P])
        x_log = sb("x_log", [P, 2 * C, S])
        x_sh = sb("x_sh", [P, 2 * C, S])
        x_p = x_pn = x_sh
        x_mx = sb("x_mx", [P, 2 * C])
        x_sum = sb("x_sum", [P, 2 * C])
        x_rs = sb("x_rs", [P, 2 * C])
        x_pT = sb("x_pT", [P, 2, 4, 2, S])
        x_aT = sb("x_aT", [P, P])
        x_keep = sb("x_keep", [P, 2, D])
        x1 = sb("x1", [P, 2, D])

        a_stat = sb("a_stat", [P, 6])
        a_mv = sb("a_mv", [P, 2])
        a_ln = sb("a_ln", [P, 2])
        a_n = sb("a_n", [P, D])
        a_hT = sb("a_hT", [P, P])
        a_hi = sb("a_hi", [P, P], F32R)
        a_lo = sb("a_lo", [P, P], F32R)
        a_sq = sb("a_sq", [P, 2, HF, S])
        a_ss = sb("a_ss", [P, 2, HF])
        a_lnss = sb("a_lnss", [P, 2, HF])
        a_r = sb("a_r", [P, 2, HF])
        a_qk = sb("a_qk", [P, 2, HF, S])
        a_qT = sb("a_qT", [P, C, P])
        a_kT = sb("a_kT", [P, C, P])
        a_v = sb("a_v", [P, 2, INNER])
        b_sh = sb("b_sh", [P, 2 * C, S])
        b_p = b_pn = b_sh
        b_mx = sb("b_mx", [P, 2 * C])
        b_sum = sb("b_sum", [P, 2 * C])
        b_rs = sb("b_rs", [P, 2 * C])
        b_pT = sb("b_pT", [P, C, 2, S])
        b_aT = sb("b_aT", [P, C, 2, S])
        b_stat = sb("b_stat", [P, 6])
        b_mv = sb("b_mv", [P, 2])
        b_ln = sb("b_ln", [P, 2])
        b_n = sb("b_n", [P, D])
        b_hT = sb("b_hT", [P, P])
        b_gl = sb("b_gl", [P, E])
        b_gm = sb("b_gm", [P, 1])
        b_ge = sb("b_ge", [P, E])
        b_gs = sb("b_gs", [P, 1])
        b_gr = sb("b_gr", [P, 1])

        RING = 4

        def over(name, shape, dt=F32):
            nonlocal shared
            t = nc.alloc_sbuf_tensor_at(name, shape, dt, offset=shared)
            size = 4
            for n in shape[1:]:
                size *= n
            shared += size
            return t

        w2_hi = over("w2_hi", [P, NK, D], F32R)
        w2_lo = over("w2_lo", [P, NK, D], F32R)
        hid = over("hid", [P, RING, GT])
        hid_hi = over("hid_hi", [P, RING, GT], F32R)
        hid_lo = over("hid_lo", [P, RING, GT], F32R)
        g_cur = over("g_cur", [P, PER * E])
        gT_hi = over("gT_hi", [E, GT], F32R)
        gT_lo = over("gT_lo", [E, GT], F32R)
        gate_row = over("gate_row", [P, 2, GT])
        e_out = over("e_out", [P, 2, GT])
        y_T = over("y_T", [P, GT])
        y_all = over("y_all", [P, TILES * D])

        consts_in = sem("consts_in")
        weights_in = sem("weights_in")
        experts_in = sem("experts_in")
        inputs_in = [sem(f"inputs_in{p}") for p in range(2)]
        setup_T, setup_cols, setup_xwT, setup_tanh = sem("setup_T"), sem("setup_cols"), sem("setup_xwT"), sem("setup_tanh")
        setup_dve, setup_split, setup_bo, w1_split = sem("setup_dve"), sem("setup_split"), sem("setup_bo"), sem("w1_split")
        names = ("xst xmv xl xr xn xT xct xc xproj xqm xkT xkm xvm xlogits xneg xmask xmax xshift xexp xsum xrs xnorm "
                 "xPT xpT xpv xaT xo x1s x1d xkeep "
                 "ast amv al ar an aT ahT ahi alo aq asq ass aln arr aqn ak ksq kss kln krr akn av avd aqT aqd aqs akT akd "
                 "bs bmax bsh bexp bsum brs bnorm bPT bpT bpv baT bo bst bmv bl br bn bT bhT bhi blo "
                 "bg bgl bgm bge bgr bgn").split()
        s = {n: sem("s_" + n) for n in names}
        hid_ps, hid_done, hid_used = sem("hid_ps"), sem("hid_done"), sem("hid_used")
        hi_done, lo_done, w2_hi_done, w2_lo_done = sem("hi_done"), sem("lo_done"), sem("w2_hi_done"), sem("w2_lo_done")
        g_cur_done, gT_ps, gT_hi_done, gT_lo_done = sem("g_cur_done"), sem("gT_ps"), sem("gT_hi_done"), sem("gT_lo_done")
        row_ps, row_done, out_done = sem("row_ps"), sem("row_done"), sem("out_done")
        acc_done, y_ps, y_done, yT_ps = sem("acc_done"), sem("y_ps"), sem("y_done"), sem("yT_ps")
        y_stats, y_mvs, y_kept, yl, yr = sem("y_stats"), sem("y_mvs"), sem("y_kept"), sem("yl"), sem("yr")
        f1, f2, f3, stored, xb_done = sem("f1"), sem("f2"), sem("f3"), sem("stored"), sem("xb_done")

        y_ag, passed = sem("y_ag"), sem("passed")

        def hold(eng, sm, value):
            ge(eng, sm, value)
            if not isinstance(value, int):
                eng.sem_inc(passed, 1)

        def done(eng, product, value, alone=False):
            if isinstance(value, int):
                if value > 0:
                    eng.wait_ge(s[product], min(value, TILES))
            elif alone:
                hold(eng, s[product], value)
            else:
                eng.wait_ge(s[product], value)

        def counts(eng, t):
            return [t + 1 - k if isinstance(t, int) else eng.snap(t + (1 - k)) for k in range(LAGS + 1)]

        def run_tiles(eng, body):
            for t in range(LAGS):
                body(t, t % 2, t)
            with eng.Fori(3, TILES // 2) as j:
                body(2 * j - 1, 1, None)
                body(2 * j, 0, None)
            for t in range(TILES - 1, TILES + LAGS - 1):
                body(t, t % 2, t)

        def inputs_of(eng, t, p):
            if isinstance(t, int):
                return 64 * (t // 2 + 1)
            return eng.snap(32 * t + (64 - 32 * p))

        def has(static, stage):
            return static is None or 0 <= static - stage < TILES

        def hid_bank(k):
            return (ps_s if k % 4 < 2 else ps_t)[:, k % 2, :]

        XA, XB, A, BA, BB = range(5)
        LAGS = 5
        flat = lambda ap: ap[:, :, :].rearrange("p a b -> p (a b)")
        block = stack.enter_context(nc.Block())

        @block.sync
        def _(sp):
            sp.dma_start(cst[:, 0:C_SEL], consts[:, 0:C_SEL]).then_inc(consts_in, 16)
            sp.dma_start(cst[0:E, C_SEL:C_END], consts[0:E, C_SEL:C_END]).then_inc(consts_in, 16)
            for j, w in enumerate((xwq, xwk, xwv, xwo)):
                sp.dma_start(xw[:, j, :], w).then_inc(consts_in, 16)
            for r, v in ((ROW_BQ, xbq), (ROW_BK, xbk), (ROW_BV, xbv), (ROW_G, ln_g), (ROW_B, ln_b)):
                sp.dma_start(rows[r:r + 1, :], row(v)).then_inc(consts_in, 16)
            sp.dma_start(rows[ROW_QS:ROW_QS + C, :], q_scale.rearrange("(c h) a d -> c (h a d)", h=2)).then_inc(consts_in, 16)
            sp.dma_start(rows[ROW_KS:ROW_KS + C, :], k_scale.rearrange("(c h) a d -> c (h a d)", h=2)).then_inc(consts_in, 16)
            sp.dma_start(rows[ROW_B1:ROWS, :], b1.rearrange("e (c f) -> (e c) f", f=P)).then_inc(consts_in, 16)

            def load(t, p):
                sp.dma_start(x_in[:, p, :], x_t[bass.ts(t, P)]).then_inc(inputs_in[p], 16)
                sp.dma_start(c_in[:, p, :], c_t[bass.ts(t, P)]).then_inc(inputs_in[p], 16)
                for h in range(2):
                    sp.dma_start(m_in[h * S:(h + 1) * S, p, :, :], m_t[:, bass.ts(t, 2), :]).then_inc(inputs_in[p], 16)

            load(0, 0)
            load(1, 1)
            for j, w in enumerate((wq, wk, wv)):
                sp.dma_start(wqkv[:, j, :], w).then_inc(weights_in, 16)
            sp.dma_start(wo_s[:, :, :], wo.rearrange("(c p) d -> p c d", p=P)).then_inc(weights_in, 16)
            sp.dma_start(gate_ws[:, :], gate_w).then_inc(weights_in, 16)
            sp.dma_start(b2_s[:, :], b2).then_inc(weights_in, 16)
            sp.wait_ge(setup_T, 4)
            sp.wait_ge(setup_split, 2)
            sp.dma_start(stage[:, :].rearrange("p (e f) -> p e f", e=E), w1.rearrange("e d f -> d e f")).then_inc(experts_in, 16)
            for t in range(2):
                sp.wait_ge(s["xmask"], t + 1)
                sp.wait_ge(s["xkeep"], t + 1)
                load(t + 2, t)
            sp.wait_ge(w1_split, 2)
            sp.dma_start(w2_s, w2.rearrange("e (c p) d -> p (e c) d", p=P)).then_inc(experts_in, 16)
            with sp.Fori(1, TILES // 2 - 1) as j:
                i = 2 * j
                for p in range(2):
                    sp.wait_ge(s["xmask"], i + (p + 1))
                    sp.wait_ge(s["xkeep"], i + (p + 1))
                    load(i + (p + 2), p)

        @block.gpsimd
        def _(pool):
            pool.wait_ge(weights_in, 96)
            pool.tensor_copy(wqkv_hi[:, :, :], wqkv[:, :, :]).then_inc(setup_split, 1)
            pool.wait_ge(setup_split, 1)
            pool.tensor_tensor(wqkv_lo[:, :, :], wqkv[:, :, :], wqkv_hi[:, :, :].bitcast(F32), ALU.subtract).then_inc(setup_split, 1)

            pool.wait_ge(setup_cols, 9)

            def body(t, p, static):
                n = counts(pool, t)
                if has(static, XA):
                    done(pool, "xshift", n[1], alone=True)
                    pool.memset(flat(x_log), NEG).then_inc(s["xneg"], 1)
                    pool.wait_ge(inputs_in[p], inputs_of(pool, t, p))
                    done(pool, "x1d", n[2])
                    pool.tensor_tensor(x_keep[:, p, :], x_in[:, p, :], tg_bo[:, :], ALU.add).then_inc(s["xkeep"], 1)
                    done(pool, "xkT", n[XA])
                    pool.tensor_tensor(xk_m[:, :, :, :], xk_T[:, :, :].unsqueeze(2).to_broadcast([P, 2, C, S]),
                                       pair_mask.unsqueeze(1).unsqueeze(3).to_broadcast([P, 2, C, S]),
                                       ALU.mult).then_inc(s["xkm"], 1)
                if has(static, BA):
                    done(pool, "brs", n[BA])
                    pool.tensor_tensor(b_pn[:, :, :], b_p[:, :, :], b_rs[:, :].unsqueeze(2).to_broadcast([P, 2 * C, S]),
                                       ALU.mult).then_inc(s["bnorm"], 1)
                if has(static, XA):
                    done(pool, "xPT", n[XB])
                    done(pool, "xmax", n[XA])
                    pool.tensor_tensor(x_sh[:, :, :], x_log[:, :, :], x_mx[:, :].unsqueeze(2).to_broadcast([P, 2 * C, S]),
                                       ALU.subtract).then_inc(s["xshift"], 1)
                if has(static, A):
                    done(pool, "aqd", n[A])
                    pool.tensor_tensor(a_qT[:, :, :], a_qT[:, :, :], qk_scale[:, :].unsqueeze(2).to_broadcast([P, C, P]),
                                       ALU.mult).then_inc(s["aqs"], 1)
                if has(static, XA):
                    done(pool, "xrs", n[XA])
                    pool.tensor_tensor(x_pn[:, :, :], x_p[:, :, :], x_rs[:, :].unsqueeze(2).to_broadcast([P, 2 * C, S]),
                                       ALU.mult).then_inc(s["xnorm"], 1)
                if static == 0:
                    pool.wait_ge(experts_in, 16)
                    pool.tensor_copy(w1_hi[:, :, :], w1_s).then_inc(w1_split, 1)
                if static == 1:
                    pool.wait_ge(w1_split, 1)
                    pool.tensor_tensor(w1_lo[:, :, :], w1_s, w1_hi[:, :, :].bitcast(F32), ALU.subtract).then_inc(w1_split, 1)
                    pool.tensor_copy(b2_hi[:, :], b2_s[:, :]).then_inc(w1_split, 1)
                    pool.wait_ge(w1_split, 3)
                    pool.tensor_tensor(b2_lo[:, :], b2_s[:, :], b2_hi[:, :].bitcast(F32), ALU.subtract).then_inc(w1_split, 1)

            run_tiles(pool, body)

            pool.wait_ge(s["blo"], TILES)
            pool.wait_ge(s["bgn"], TILES)
            pool.wait_ge(experts_in, 32)
            for e in range(E):
                pool.tensor_copy(w2_hi[:, 4 * e:4 * e + 4, :], w2_s[:, 4 * e:4 * e + 4, :]).then_inc(w2_hi_done, 1)

            def experts(g, first):
                for e in range(E):
                    add_expert(g, e, first)

            def add_expert(g, e, first):
                ge(pool, out_done, g * E + (e + 1))
                if e == 0:
                    if not first:
                        hold(pool, y_kept, g)
                    ins = pool.tensor_copy(y_T[:, :], e_out[:, e % 2, :])
                else:
                    ge(pool, acc_done, g * E + e)
                    ins = pool.tensor_tensor(y_T[:, :], y_T[:, :], e_out[:, e % 2, :], ALU.add)
                ins.then_inc(acc_done, 1)

            experts(0, True)
            with pool.Fori(1, GROUPS) as g:
                experts(g, False)

        @block.scalar
        def _(act):
            for tile, v in ((bo_b, xbo), (g_b, ln_g), (b_b, ln_b), (gate_bb, gate_b)):
                act.dma_start(tile[:, :], v.partition_broadcast(P)).then_inc(setup_bo, 16)
            for j, v in enumerate((g_xattn, g_ffn)):
                act.dma_start(gates_in[:, j:j + 1], v.partition_broadcast(P)).then_inc(setup_bo, 16)
            act.wait_ge(setup_bo, 96)
            act.activation(tanh_g[:, :], gates_in[:, :], ACT.Tanh).then_inc(setup_tanh, 1)
            act.wait_ge(setup_T, 4)
            act.copy(flat(xwT), ps_s[:, 0, :]).then_inc(setup_xwT, 1)
            act.wait_ge(setup_dve, 3)
            act.preload_act_table_set("natural_log_exp_and_others")

            def body(t, p, static):
                n = counts(act, t)
                if has(static, XA):
                    done(act, "xmv", n[XA])
                    act.activation(x_ln[:, 0:1], x_mv[:, 1:2], ACT.Ln, bias=eps2[:, 0:1]).then_inc(s["xl"], 1)
                    done(act, "xl", n[XA])
                    act.activation(x_ln[:, 1:2], x_ln[:, 0:1], ACT.Exp, scale=-0.5).then_inc(s["xr"], 1)
                if has(static, A):
                    done(act, "amv", n[A])
                    act.activation(a_ln[:, 0:1], a_mv[:, 1:2], ACT.Ln, scale=1.0 + EPS, bias=eps2[:, 1:2]).then_inc(s["al"], 1)
                    done(act, "al", n[A])
                    act.activation(a_ln[:, 1:2], a_ln[:, 0:1], ACT.Exp, scale=-0.5).then_inc(s["ar"], 1)
                    done(act, "aT", n[A])
                    act.activation(a_hT[:, :], ps_y[:, 0:P], ACT.Identity, scale=cols[:, ROW_G:ROW_G + 1],
                                   bias=cols[:, ROW_B:ROW_B + 1]).then_inc(s["ahT"], 1)
                if has(static, XA):
                    done(act, "xT", n[XA])
                    act.copy(xnT[:, :], ps_x[:, 0:P]).then_inc(s["xct"], 1)
                    act.copy(ctxT[:, :, :, :], ps_x[:, P:2 * P].rearrange("p (b k) -> p b k", b=2).unsqueeze(2)
                             .to_broadcast([P, 2, 2, S])).then_inc(s["xc"], 1)
                if has(static, BB):
                    done(act, "bPT", n[BB])
                    act.copy(b_pT[:, :, :, :].rearrange("p c h q -> p (c h q)"), flat(ps_t)).then_inc(s["bpT"], 1)
                if has(static, XA):
                    done(act, "xproj", n[XA])
                    act.activation(xk_T[:, :, :].rearrange("p b k -> p (b k)"), ps_x[:, P:2 * P], ACT.Identity,
                                   bias=cols[:, ROW_BK:ROW_BK + 1]).then_inc(s["xkT"], 1)
                    for h in range(2):
                        last = act.activation(xq_m[:, :, h, :], ps_x[:, 0:P].rearrange("p (b q) -> p b q", b=2), ACT.Identity,
                                              scale=par_mask[:, h:h + 1], bias=bq_par[:, h:h + 1])
                    last.then_inc(s["xqm"], 1)
                if has(static, A):
                    done(act, "ahT", n[A])
                    act.copy(a_hi[:, :], a_hT[:, :]).then_inc(s["ahi"], 1)
                if has(static, XB):
                    done(act, "xPT", n[XB])
                    act.copy(x_pT[:, :, :, :, :].rearrange("p b j h q -> p (b j h q)"), flat(ps_t)).then_inc(s["xpT"], 1)
                if has(static, BA):
                    done(act, "bsh", n[BA])
                    act.activation(flat(b_p), flat(b_sh), ACT.Exp).then_inc(s["bexp"], 1)
                if has(static, BB):
                    done(act, "bpv", n[BB])
                    act.copy(b_aT[:, :, :, :], ps_s[:, :, :].rearrange("p b (c q) -> p c b q", c=C)).then_inc(s["baT"], 1)
                if has(static, A):
                    done(act, "aq", n[A])
                    act.activation(a_sq[:, 0, :, :].rearrange("p h d -> p (h d)"), flat(ps_q), ACT.Square).then_inc(s["asq"], 1)
                    done(act, "ass", n[A])
                    act.activation(a_lnss[:, 0, :], a_ss[:, 0, :], ACT.Ln, bias=eps2[:, 2:3]).then_inc(s["aln"], 1)
                    done(act, "aln", n[A])
                    act.activation(a_r[:, 0, :], a_lnss[:, 0, :], ACT.Exp, scale=-0.5).then_inc(s["arr"], 1)
                if has(static, BB):
                    done(act, "bmv", n[BB])
                    act.activation(b_ln[:, 0:1], b_mv[:, 1:2], ACT.Ln, bias=eps2[:, 0:1]).then_inc(s["bl"], 1)
                    done(act, "bl", n[BB])
                    act.activation(b_ln[:, 1:2], b_ln[:, 0:1], ACT.Exp, scale=-0.5).then_inc(s["br"], 1)
                if has(static, A):
                    done(act, "ak", n[A])
                    act.activation(a_sq[:, 1, :, :].rearrange("p h d -> p (h d)"), flat(ps_q), ACT.Square).then_inc(s["ksq"], 1)
                if has(static, XB):
                    done(act, "xpv", n[XB])
                    act.activation(x_aT[:, :], ps_x[:, 0:P], ACT.Identity, bias=cols[:, ROW_BV:ROW_BV + 1]).then_inc(s["xaT"], 1)
                if has(static, A):
                    done(act, "aqT", n[A])
                    act.copy(flat(a_qT), flat(ps_t)).then_inc(s["aqd"], 1)
                    done(act, "kss", n[A])
                    act.activation(a_lnss[:, 1, :], a_ss[:, 1, :], ACT.Ln, bias=eps2[:, 2:3]).then_inc(s["kln"], 1)
                    done(act, "kln", n[A])
                    act.activation(a_r[:, 1, :], a_lnss[:, 1, :], ACT.Exp, scale=-0.5).then_inc(s["krr"], 1)
                if has(static, BB):
                    done(act, "bT", n[BB])
                    act.activation(b_hT[:, :], ps_y[:, 0:P], ACT.Identity, scale=cols[:, ROW_G:ROW_G + 1],
                                   bias=cols[:, ROW_B:ROW_B + 1]).then_inc(s["bhT"], 1)
                if has(static, XA):
                    done(act, "xshift", n[XA])
                    act.activation(flat(x_p), flat(x_sh), ACT.Exp).then_inc(s["xexp"], 1)
                if has(static, A):
                    done(act, "akT", n[A])
                    act.copy(flat(a_kT), flat(ps_t)).then_inc(s["akd"], 1)
                    done(act, "bpv", n[BB])
                    done(act, "av", n[A])
                    act.copy(a_v[:, p, :], flat(ps_q)).then_inc(s["avd"], 1)
                if has(static, BB):
                    done(act, "bhT", n[BB], alone=True)
                    act.copy(h_hi[:, bass.ts(t - BB, P)], b_hT[:, :]).then_inc(s["bhi"], 1)
                    done(act, "bgm", n[BB])
                    act.activation(b_ge[:, :], b_gl[:, :], ACT.Exp, bias=b_gm[:, 0:1], accum_out=b_gs[:, 0:1]).then_inc(s["bge"], 1)

            run_tiles(act, body)

            def gelu(g, k):
                ge(act, hid_ps, g * NK + (k + 1))
                if isinstance(g, int) and g == 0:
                    ge(act, lo_done, k + 1 - RING)
                else:
                    act.wait_ge(lo_done, g * NK + (k + 1 - RING))
                act.activation(hid[:, k % RING, :], hid_bank(k), ACT.Gelu_apprx_tanh,
                               bias=cols[:, ROW_B1 + k:ROW_B1 + k + 1]).then_inc(hid_done, 1)

            def keep_gate(g, e, first):
                ge(act, row_ps, g * E + (e + 1))
                if first:
                    ge(act, out_done, e - 1)
                else:
                    act.wait_ge(out_done, g * E + (e - 1))
                act.copy(gate_row[:, e % 2, :], ps_x[:, :]).then_inc(row_done, 1)

            for k in range(NK):
                gelu(0, k)
                if k % 4 == 3:
                    keep_gate(0, k // 4, True)
            with act.Fori(1, GROUPS) as g:
                for k in range(NK):
                    gelu(g, k)
                    if k % 4 == 3:
                        keep_gate(g, k // 4, False)
            act.preload_act_table_set("natural_log_exp_and_others")
            act.wait_ge(y_mvs, GROUPS)
            act.activation(y_ln[:, :], y_mv[:, :, 1], ACT.Ln, bias=eps2[:, 0:1]).then_inc(yl, 1)
            act.wait_ge(yl, 1)
            act.activation(y_r[:, :], y_ln[:, :], ACT.Exp, scale=-0.5).then_inc(yr, 1)
            for c in range(GROUPS):
                act.wait_ge(f3, c + 1)
                act.dma_start(out_t[:, c * PER:(c + 1) * PER, :], y_all[:, c * PER * D:(c + 1) * PER * D]
                              .rearrange("p (t d) -> p t d", d=D)).then_inc(stored, 16)
            act.wait_ge(stored, 16 * GROUPS)

        @block.vector
        def _(dve):
            for j, e in enumerate((EPS, EPS * EPS, 1e-12)):
                dve.memset(eps2[:, j:j + 1], e).then_inc(setup_dve, 1)
            dve.wait_ge(setup_T, 5)
            dve.tensor_copy(cols[:, :], ps_x[:, 0:ROWS]).then_inc(setup_cols, 1)
            dve.wait_ge(setup_cols, 1)
            dve.scalar_tensor_tensor(qk_scale[:, :], cols[:, ROW_QS:ROW_QS + C], 10.0, cols[:, ROW_KS:ROW_KS + C],
                                     ALU.mult, ALU.mult).then_inc(setup_cols, 1)
            dve.tensor_copy(sel[:, :], cst[0:E, C_SEL:C_END]).then_inc(setup_cols, 1)
            dve.wait_ge(setup_tanh, 1)
            dve.tensor_scalar(tg_bo[:, :], bo_b[:, :], tanh_g[:, 0:1], None, ALU.mult).then_inc(setup_cols, 1)
            dve.tensor_scalar(tg_g[:, :], g_b[:, :], tanh_g[:, 1:2], None, ALU.mult).then_inc(setup_cols, 1)
            dve.tensor_scalar(tg_b[:, :], b_b[:, :], tanh_g[:, 1:2], None, ALU.mult).then_inc(setup_cols, 1)
            dve.tensor_copy(ident_r[:, :], ident).then_inc(setup_cols, 1)
            dve.tensor_copy(causal_r[:, :, :], causal.unsqueeze(1).to_broadcast([P, C, S])).then_inc(setup_cols, 1)
            dve.tensor_scalar(bq_par[:, :], par_mask, cols[:, ROW_BQ:ROW_BQ + 1], None, ALU.mult).then_inc(setup_cols, 1)

            def body(t, p, static):
                n = counts(dve, t)
                q = 1 - p
                if has(static, A):
                    done(dve, "x1s", n[A])
                    dve.bn_stats(a_stat[:, :], x1[:, p, :]).then_inc(s["ast"], 1)
                if has(static, XA):
                    dve.wait_ge(inputs_in[p], inputs_of(dve, t, p))
                    dve.bn_stats(x_stat[:, :], x_in[:, p, :]).then_inc(s["xst"], 1)
                if has(static, A):
                    done(dve, "ast", n[A], alone=True)
                    dve.bn_aggr(a_mv[:, :], a_stat[:, :]).then_inc(s["amv"], 1)
                if has(static, XA):
                    done(dve, "xst", n[XA], alone=True)
                    dve.bn_aggr(x_mv[:, :], x_stat[:, :]).then_inc(s["xmv"], 1)
                    done(dve, "xr", n[XA])
                    dve.tensor_scalar(x_n[:, :], x_in[:, p, :], x_mv[:, 0:1], x_ln[:, 1:2], ALU.subtract,
                                      ALU.mult).then_inc(s["xn"], 1)
                if has(static, A):
                    done(dve, "ar", n[A])
                    dve.tensor_scalar(a_n[:, :], x1[:, p, :], a_mv[:, 0:1], a_ln[:, 1:2], ALU.subtract,
                                      ALU.mult).then_inc(s["an"], 1)
                if has(static, BA):
                    done(dve, "bs", n[BA])
                    b_log = ps_s[:, :, :].rearrange("p a (c k) -> p (a c) k", k=S)
                    dve.tensor_reduce(b_mx[:, :], b_log, AX_X, ALU.max).then_inc(s["bmax"], 1)
                    done(dve, "bPT", n[BB])
                    done(dve, "bmax", n[BA])
                    dve.tensor_tensor(b_sh[:, :, :], b_log, b_mx[:, :].unsqueeze(2).to_broadcast([P, 2 * C, S]),
                                      ALU.subtract).then_inc(s["bsh"], 1)
                if has(static, A):
                    done(dve, "ahi", n[A])
                    dve.tensor_tensor(a_lo[:, :], a_hT[:, :], a_hi[:, :].bitcast(F32), ALU.subtract).then_inc(s["alo"], 1)
                if has(static, XA):
                    done(dve, "xqm", n[XA])
                    dve.tensor_tensor(xv_m[:, p, :, :, :], ps_x[:, 2 * P:4 * P].rearrange("p (b f) -> p b f", b=2).unsqueeze(2)
                                      .to_broadcast([P, 2, 2, P]), v_mask.unsqueeze(1).to_broadcast([P, 2, 2, P]),
                                      ALU.mult).then_inc(s["xvm"], 1)
                if has(static, BA):
                    done(dve, "bexp", n[BA])
                    dve.tensor_reduce(b_sum[:, :], b_p[:, :, :], AX_X, ALU.add).then_inc(s["bsum"], 1)
                if has(static, A):
                    done(dve, "asq", n[A])
                    dve.tensor_reduce(a_ss[:, 0, :], a_sq[:, 0, :, :], AX_X, ALU.add).then_inc(s["ass"], 1)
                if has(static, BA):
                    done(dve, "bsum", n[BA])
                    dve.reciprocal(b_rs[:, :], b_sum[:, :]).then_inc(s["brs"], 1)
                if has(static, BB):
                    done(dve, "bo", n[BB])
                    dve.bn_stats(b_stat[:, :], ps_y[:, 0:D]).then_inc(s["bst"], 1)
                    done(dve, "bst", n[BB], alone=True)
                    dve.bn_aggr(b_mv[:, :], b_stat[:, :]).then_inc(s["bmv"], 1)
                if has(static, A):
                    done(dve, "arr", n[A])
                    dve.tensor_tensor(a_qk[:, 0, :, :], ps_q[:, :, :].rearrange("p a (h d) -> p (a h) d", d=S),
                                      a_r[:, 0, :].unsqueeze(2).to_broadcast([P, HF, S]), ALU.mult).then_inc(s["aqn"], 1)
                if has(static, XA):
                    done(dve, "xneg", n[XA])
                    done(dve, "xlogits", n[XA], alone=True)
                    for b in range(2):
                        last = dve.copy_predicated(x_log[:, b * C:(b + 1) * C, :], m_in[:, p, b, :].unsqueeze(1)
                                                   .to_broadcast([P, C, S]), ps_s[:, b, :].rearrange("p (c k) -> p c k", k=S))
                    last.then_inc(s["xmask"], 1)
                    done(dve, "xmask", n[XA])
                    dve.tensor_reduce(x_mx[:, :], x_log[:, :, :], AX_X, ALU.max).then_inc(s["xmax"], 1)
                if has(static, A):
                    done(dve, "ksq", n[A])
                    dve.tensor_reduce(a_ss[:, 1, :], a_sq[:, 1, :, :], AX_X, ALU.add).then_inc(s["kss"], 1)
                if has(static, BB):
                    done(dve, "br", n[BB])
                    dve.tensor_scalar(b_n[:, :], ps_y[:, 0:D], b_mv[:, 0:1], b_ln[:, 1:2], ALU.subtract,
                                      ALU.mult).then_inc(s["bn"], 1)
                if has(static, A):
                    done(dve, "krr", n[A])
                    dve.tensor_tensor(a_qk[:, 1, :, :], ps_q[:, :, :].rearrange("p a (h d) -> p (a h) d", d=S),
                                      a_r[:, 1, :].unsqueeze(2).to_broadcast([P, HF, S]), ALU.mult).then_inc(s["akn"], 1)
                if has(static, XA):
                    done(dve, "xexp", n[XA])
                    dve.tensor_reduce(x_sum[:, :], x_p[:, :, :], AX_X, ALU.add).then_inc(s["xsum"], 1)
                    done(dve, "xsum", n[XA])
                    dve.reciprocal(x_rs[:, :], x_sum[:, :]).then_inc(s["xrs"], 1)
                if has(static, BB):
                    done(dve, "bg", n[BB])
                    dve.tensor_tensor(b_gl[:, :], ps_y[:, 0:E], gate_bb[:, :], ALU.add).then_inc(s["bgl"], 1)
                if has(static, XB):
                    done(dve, "xo", n[XB])
                    dve.scalar_tensor_tensor(x1[:, q, :], ps_x[:, P:2 * P], tanh_g[:, 0:1], x_keep[:, q, :], ALU.mult,
                                             ALU.add).then_inc(s["x1s"], 1)
                    dve.scalar_tensor_tensor(x1_all[:, bass.ts(t - XB, D)], ps_x[:, P:2 * P], tanh_g[:, 0:1], x_keep[:, q, :],
                                             ALU.mult, ALU.add).then_inc(s["x1d"], 1)
                if has(static, BB):
                    done(dve, "bgl", n[BB])
                    dve.tensor_reduce(b_gm[:, :], b_gl[:, :], AX_X, ALU.max, negate=True).then_inc(s["bgm"], 1)
                    done(dve, "bhi", n[BB])
                    dve.tensor_tensor(h_lo[:, bass.ts(t - BB, P)], b_hT[:, :], h_hi[:, bass.ts(t - BB, P)].bitcast(F32),
                                      ALU.subtract).then_inc(s["blo"], 1)
                    done(dve, "bge", n[BB])
                    dve.reciprocal(b_gr[:, :], b_gs[:, :]).then_inc(s["bgr"], 1)
                    done(dve, "bgr", n[BB])
                    dve.tensor_scalar(gates[:, bass.ts(t - BB, E)], b_ge[:, :], b_gr[:, 0:1], None, ALU.mult).then_inc(s["bgn"], 1)

            run_tiles(dve, body)

            dve.wait_ge(w2_hi_done, E)
            for e in range(E):
                dve.tensor_tensor(w2_lo[:, 4 * e:4 * e + 4, :], w2_s[:, 4 * e:4 * e + 4, :],
                                  w2_hi[:, 4 * e:4 * e + 4, :].bitcast(F32), ALU.subtract).then_inc(w2_lo_done, 1)

            def weigh(g, e, first):
                ge(dve, hid_used, g * NK + (4 * e + 4))
                ge(dve, row_done, g * E + (e + 1))
                if first:
                    ge(dve, acc_done, e - 1)
                else:
                    dve.wait_ge(acc_done, g * E + (e - 1))
                dve.tensor_tensor(e_out[:, e % 2, :], ps_q[:, e % 2, :], gate_row[:, e % 2, :], ALU.mult).then_inc(out_done, 1)

            def experts(g, first):
                if not first:
                    dve.wait_ge(gT_ps, g)
                dve.tensor_copy(g_cur[:, :], gates[:, bass.ts(g, PER * E)]).then_inc(g_cur_done, 1)
                for k in range(NK):
                    if k == 0:
                        ge(dve, gT_ps, g + 1)
                        dve.tensor_copy(gT_hi[:, :], ps_y[0:E, :]).then_inc(gT_hi_done, 1)
                        ge(dve, gT_hi_done, g + 1)
                        dve.tensor_tensor(gT_lo[:, :], ps_y[0:E, :], gT_hi[:, :].bitcast(F32), ALU.subtract).then_inc(gT_lo_done, 1)
                    ge(dve, hid_done, g * NK + (k + 1))
                    if first:
                        hold(dve, hid_used, k + 1 - RING)
                    else:
                        hold(dve, hid_used, g * NK + (k + 1 - RING))
                    dve.tensor_copy(hid_hi[:, k % RING, :], hid[:, k % RING, :]).then_inc(hi_done, 1)
                    ge(dve, hi_done, g * NK + (k + 1))
                    dve.tensor_tensor(hid_lo[:, k % RING, :], hid[:, k % RING, :], hid_hi[:, k % RING, :].bitcast(F32),
                                      ALU.subtract).then_inc(lo_done, 1)
                    if k % 4 == 3 and k > 4:
                        weigh(g, k // 4 - 1, first)
                weigh(g, E - 1, first)
                ge(dve, acc_done, g * E + E)
                ge(dve, y_ps, g + 1)
                dve.tensor_tensor(y_T[:, :], ps_y[:, :], y_T[:, :], ALU.add).then_inc(y_done, 1)
                ge(dve, yT_ps, g + 1)
                for c in range(PER):
                    dve.bn_stats(y_stat[:, c, :], ps_y[:, c * P:(c + 1) * P]).then_inc(y_stats, 1)
                dve.tensor_copy(y_all[:, bass.ts(g, PER * D)], ps_y[:, :]).then_inc(y_kept, 1)
                hold(dve, y_stats, g * PER + PER)
                for c in range(PER):
                    ins = dve.bn_aggr(y_mg[:, c, :], y_stat[:, c, :]).then_inc(y_ag, 1)
                ge(dve, y_ag, g * PER + PER)
                dve.tensor_copy(flat(y_mv)[:, bass.ts(g, PER * 2)], flat(y_mg)).then_inc(y_mvs, 1)

            experts(0, True)
            with dve.Fori(1, GROUPS) as g:
                experts(g, False)
            dve.wait_ge(yr, 1)
            for c in range(TILES):
                yc = y_all[:, c * D:(c + 1) * D]
                dve.tensor_scalar(yc, yc, y_mv[:, c, 0:1], y_r[:, c:c + 1], ALU.subtract, ALU.mult).then_inc(f1, 1)
            for g in range(GROUPS):
                w = slice(g * PER * D, (g + 1) * PER * D)
                y3 = y_all[:, w].rearrange("p (t d) -> p t d", d=D)
                x3 = x1_all[:, w].rearrange("p (t d) -> p t d", d=D)
                dve.wait_ge(f1, TILES)
                dve.tensor_tensor(y3, y3, tg_g[:, :].unsqueeze(1).to_broadcast([P, PER, D]), ALU.mult).then_inc(f2, 1)
                dve.tensor_tensor(x3, x3, tg_b[:, :].unsqueeze(1).to_broadcast([P, PER, D]), ALU.add).then_inc(f2, 1)
                dve.wait_ge(f2, 2 * g + 2)
                dve.tensor_tensor(y3, y3, x3, ALU.add).then_inc(f3, 1)

        @block.tensor
        def _(pe):
            pe.wait_ge(consts_in, 16 * 14)
            for j in range(4):
                pe.transpose(ps_s[:, 0, j * P:(j + 1) * P], xw[:, j, :], ident).then_inc(setup_T, 1)
            pe.transpose(ps_x[:, 0:ROWS], rows[:, :], cst[0:ROWS, C_ID:C_ID + ROWS]).then_inc(setup_T, 1)
            pe.wait_ge(setup_xwT, 1)
            pe.wait_ge(setup_cols, 9)

            def split_mm(o, l_hi, l_lo, r_hi, r_lo, start=True, stop=True):
                pe.matmul(o, l_hi, r_hi, start=start, stop=False)
                pe.matmul(o, l_hi, r_lo, start=False, stop=False)
                return pe.matmul(o, l_lo, r_hi, start=False, stop=stop)

            def transposes(of):
                for c in range(C):
                    last = pe.transpose(ps_t[:, c // 4, (c % 4) * P:(c % 4 + 1) * P], of(c), ident)
                return last

            def project(j):
                for k in range(2):
                    w = slice(k * 512, (k + 1) * 512)
                    last = split_mm(ps_q[:, k, :], a_hi[:, :], a_lo[:, :], wqkv_hi[:, j, w], wqkv_lo[:, j, w])
                return last

            def body(t, p, static):
                n = counts(pe, t)
                q = 1 - p
                if has(static, BA):
                    done(pe, "xmask", n[1])
                    done(pe, "aqs", n[BA])
                    done(pe, "akd", n[BA])
                    for k in range(2):
                        pe.matmul(ps_s[:, k, :], ident_r[:, :], causal_r[:, :, :].rearrange("p c k -> p (c k)"),
                                  start=True, stop=True)
                    for c in range(C):
                        for b in range(2):
                            for h in range(2):
                                o = ps_s[h * S:(h + 1) * S, c // 4, (c % 4) * P + b * S:(c % 4) * P + (b + 1) * S]
                                last = pe.matmul(o, a_qT[h * S:(h + 1) * S, c, b * S:(b + 1) * S],
                                                 a_kT[h * S:(h + 1) * S, c, b * S:(b + 1) * S], start=False, stop=True,
                                                 skip_group_check=True)
                    last.then_inc(s["bs"], 1)
                if has(static, A):
                    done(pe, "bgl", n[BB + 1])
                    done(pe, "an", n[A])
                    pe.transpose(ps_y[:, 0:P], a_n[:, :], ident).then_inc(s["aT"], 1)
                if has(static, XA):
                    done(pe, "x1d", n[XB + 1])
                    done(pe, "xn", n[XA])
                    pe.transpose(ps_x[:, 0:P], x_n[:, :], ident)
                    pe.transpose(ps_x[:, P:2 * P], c_in[:, p, :], ident).then_inc(s["xT"], 1)
                if has(static, BB):
                    done(pe, "akd", n[A + 1])
                    done(pe, "bnorm", n[BB])
                    transposes(lambda c: b_pn[:, 2 * c:2 * c + 2, :].rearrange("p b k -> p (b k)")).then_inc(s["bPT"], 1)
                if has(static, XA):
                    done(pe, "xc", n[XA])
                    pe.matmul(ps_x[:, 0:P], xwT[:, 0, :], xnT[:, :], start=True, stop=True)
                    pe.matmul(ps_x[:, P:2 * P], xwT[:, 1, :], ctxT[:, :, 0, :], start=True, stop=True)
                    for b in range(2):
                        last = pe.matmul(ps_x[:, (2 + b) * P:(3 + b) * P], ctxT[:, b, :, :].rearrange("p a k -> p (a k)"),
                                         xwT[:, 2, :], start=True, stop=True)
                    last.then_inc(s["xproj"], 1)
                if has(static, XB):
                    done(pe, "bpT", n[BB])
                    done(pe, "xnorm", n[XB])
                    transposes(lambda c: x_pn[:, 2 * c:2 * c + 2, :].rearrange("p c k -> p (c k)")).then_inc(s["xPT"], 1)
                if has(static, BB):
                    done(pe, "avd", n[BB], alone=True)
                    done(pe, "bpT", n[BB], alone=True)
                    done(pe, "bsh", n[BA], alone=True)
                    for c in range(C):
                        for h in range(2):
                            for b in range(2):
                                last = pe.matmul(ps_s[h * S:(h + 1) * S, b, c * S:(c + 1) * S],
                                                 a_v[b * S:(b + 1) * S, p, (2 * c + h) * S:(2 * c + h + 1) * S],
                                                 b_pT[b * S:(b + 1) * S, c, h, :], start=True, stop=True)
                    last.then_inc(s["bpv"], 1)
                if has(static, A):
                    if static == A:
                        pe.wait_ge(setup_split, 2)
                    done(pe, "avd", n[A + 1])
                    done(pe, "alo", n[A])
                    project(0).then_inc(s["aq"], 1)
                if has(static, BB):
                    done(pe, "ahT", n[A])
                    done(pe, "baT", n[BB])
                    for c in range(C):
                        last = pe.matmul(ps_y[:, 0:D], b_aT[:, c, :, :].rearrange("p b q -> p (b q)"), wo_s[:, c, :],
                                         start=(c == 0), stop=(c == C - 1))
                    last.then_inc(s["bo"], 1)
                if has(static, XA):
                    done(pe, "baT", n[BB])
                    done(pe, "bsh", n[BA])
                    done(pe, "xmask", n[1])
                    done(pe, "xkm", n[XA])
                    done(pe, "xqm", n[XA])
                    for b in range(2):
                        last = pe.matmul(ps_s[:, b, :], xq_m[:, b, :, :].rearrange("p h q -> p (h q)"),
                                         xk_m[:, b, :, :].rearrange("p c k -> p (c k)"), start=True, stop=True)
                    last.then_inc(s["xlogits"], 1)
                if has(static, A):
                    done(pe, "aqn", n[A])
                    project(1).then_inc(s["ak"], 1)
                if has(static, XB):
                    done(pe, "xvm", n[XB])
                    done(pe, "xvm", n[XA])
                    done(pe, "xpT", n[XB])
                    for b in range(2):
                        for j in range(4):
                            for h in range(2):
                                last = pe.matmul(ps_x[32 * j:32 * (j + 1), b * S:(b + 1) * S],
                                                 xv_m[:, q, b, h, 32 * j:32 * (j + 1)], x_pT[:, b, j, h, :],
                                                 start=(h == 0), stop=(h == 1))
                    last.then_inc(s["xpv"], 1)
                if has(static, A):
                    done(pe, "xpT", n[XB])
                    done(pe, "aqn", n[A])
                    transposes(lambda c: a_qk[:, 0, 2 * c:2 * c + 2, :].rearrange("p h d -> p (h d)")).then_inc(s["aqT"], 1)
                if has(static, XB):
                    done(pe, "xaT", n[XB])
                    pe.matmul(ps_x[:, P:2 * P], x_aT[:, :], xwT[:, 3, :], start=True, stop=True).then_inc(s["xo"], 1)
                if has(static, BB):
                    done(pe, "bn", n[BB])
                    pe.transpose(ps_y[:, 0:P], b_n[:, :], ident).then_inc(s["bT"], 1)
                    done(pe, "bhT", n[BB])
                    pe.matmul(ps_y[:, 0:E], b_hT[:, :], gate_ws[:, :], start=True, stop=True).then_inc(s["bg"], 1)
                if has(static, A):
                    done(pe, "aqd", n[A])
                    done(pe, "akn", n[A])
                    transposes(lambda c: a_qk[:, 1, 2 * c:2 * c + 2, :].rearrange("p h d -> p (h d)")).then_inc(s["akT"], 1)
                    project(2).then_inc(s["av"], 1)

            run_tiles(pe, body)

            LAG = 3

            def experts(g, first):
                tok = bass.ts(g, GT)
                for k in range(NK + LAG):
                    if k < NK:
                        if first:
                            ge(pe, hid_done, k + 1 - RING)
                        else:
                            pe.wait_ge(hid_done, g * NK + (k + 1 - RING))
                        split_mm(hid_bank(k), w1_hi[:, k, :], w1_lo[:, k, :], h_hi[:, tok], h_lo[:, tok]).then_inc(hid_ps, 1)
                    if k == 0:
                        ge(pe, g_cur_done, g + 1)
                        if not first:
                            pe.wait_ge(y_kept, g)
                        for c in range(PER):
                            last = pe.transpose(ps_y[0:E, c * P:(c + 1) * P], g_cur[:, c * E:(c + 1) * E], ident)
                        last.then_inc(gT_ps, 1)
                    if k % 4 == 2 and k < NK:
                        e = k // 4
                        ge(pe, gT_lo_done, g + 1)
                        if first:
                            ge(pe, row_done, e)
                        else:
                            pe.wait_ge(row_done, g * E + e)
                        pe.matmul(ps_x[:, :], sel[:, e * P:(e + 1) * P], gT_hi[:, :], start=True, stop=False)
                        pe.matmul(ps_x[:, :], sel[:, e * P:(e + 1) * P], gT_lo[:, :], start=False, stop=True).then_inc(row_ps, 1)
                    if k >= LAG:
                        j = k - LAG
                        e = j // 4
                        if j % 4 == 0:
                            if first:
                                ge(pe, out_done, e - 1)
                                pe.wait_ge(w2_lo_done, e + 1)
                            else:
                                pe.wait_ge(out_done, g * E + (e - 1))
                        ge(pe, lo_done, g * NK + (j + 1))
                        mm = split_mm(ps_q[:, e % 2, :], w2_hi[:, j, :], w2_lo[:, j, :], hid_hi[:, j % RING, :],
                                      hid_lo[:, j % RING, :], start=(j % 4 == 0), stop=(j % 4 == 3))
                        mm.then_inc(hid_used, 1)
                split_mm(ps_y[:, :], b2_hi[:, :], b2_lo[:, :], gT_hi[:, :], gT_lo[:, :]).then_inc(y_ps, 1)
                ge(pe, y_done, g + 1)
                for c in range(PER):
                    last = pe.transpose(ps_y[:, c * P:(c + 1) * P], y_T[:, c * P:(c + 1) * P], ident)
                last.then_inc(yT_ps, 1)

            pe.wait_ge(w1_split, 4)
            pe.wait_ge(s["blo"], TILES)
            pe.wait_ge(s["akd"], TILES)
            experts(0, True)
            with pe.Fori(1, GROUPS) as g:
                experts(g, False)


_INS = ['x', 'ctx_1024', 'mask_BxSxS2_if1', 'g_xattn', 'g_ffn', 'L0_xattn_Wq', 'L0_xattn_bq', 'L0_xattn_Wk', 'L0_xattn_bk',
        'L0_xattn_Wv', 'L0_xattn_bv', 'L0_xattn_Wo', 'L0_xattn_bo', 'L0_ffn_ln_g', 'L0_ffn_ln_b', 'L0_ffn_Wq', 'L0_ffn_Wk',
        'L0_ffn_Wv', 'L0_ffn_q_scale', 'L0_ffn_k_scale', 'L0_ffn_Wo', 'L0_ffn_gate_w', 'L0_ffn_gate_b', 'L0_ffn_w1',
        'L0_ffn_b1', 'L0_ffn_w2', 'L0_ffn_b2']


def _constants(np):
    t = np.zeros((P, C_END), np.float32)
    i = np.arange(P)
    t[i, C_ID + i] = 1.0
    t[:, C_CAUSAL:C_CAUSAL + S] = np.where(np.arange(S)[None, :] <= (i % S)[:, None], 0.0, NEVER)
    head = i // (D // HX)
    for h in range(2):
        t[:, C_PAR + h] = (head % 2 == h) / np.sqrt(np.float32(D // HX))
        t[:, C_VM + h * P:C_VM + (h + 1) * P] = (head % 2 == h)[None, :] & ((head // 2 % 2)[None, :] == (i // S)[:, None])
    for c in range(C):
        t[:, C_PAIR + c] = head // 2 == c
    for e in range(E):
        t[e, C_SEL + e * P:C_SEL + (e + 1) * P] = 1.0
    return t


def kernel(**inputs):
    import numpy as _np
    import concourse.bacc as _bacc
    from concourse import mybir as _mybir
    from concourse.bass_utils import run_bass_kernel_spmd as _run

    nc = _bacc.Bacc("TRN2", target_bir_lowering=False, num_devices=1)
    arrays = {"in_constants_dram": _constants(_np)}
    args = [nc.dram_tensor("in_constants_dram", (P, C_END), _mybir.dt.float32, kind="ExternalInput").ap()]
    for name in _INS:
        a = _np.ascontiguousarray(inputs[name])
        arrays[f"in_{name}_dram"] = a
        args.append(nc.dram_tensor(f"in_{name}_dram", a.shape, _mybir.dt.from_np(a.dtype), kind="ExternalInput").ap())
    out = nc.dram_tensor("out_0_dram", inputs["x"].shape, _mybir.dt.float32, kind="ExternalOutput").ap()
    gated_block(nc, *args, out)
    r = _run(nc, [arrays], core_ids=[0])
    return r.results[0]["out_0_dram"]
```

```python
from contextlib import ExitStack

import concourse.bass as bass
from concourse import mybir

F32 = mybir.dt.float32
F32R = mybir.dt.float32r
I32 = mybir.dt.int32
ALU = mybir.AluOpType
ACT = mybir.ActivationFunctionType
AX_X = mybir.AxisListType.X

P = 128
S = 64
D = 128
HX = 16
HF = 16
C = 8
INNER = 1024
E = 8
FF = 512
NK = E * FF // P
GT = 512
EPS = 1e-5
NEG = -1e9
NEVER = -2.0 ** 30

ROW_BQ, ROW_BK, ROW_BV, ROW_G, ROW_B, ROW_QS, ROW_KS, ROW_B1 = 0, 1, 2, 3, 4, 5, 13, 21
ROWS = ROW_B1 + NK

C_ID, C_CAUSAL, C_PAR, C_PAIR, C_VM, C_END = 0, 128, 192, 194, 202, 458


def gated_block(nc, consts, x, ctx_in, mask, g_xattn, g_ffn, xwq, xbq, xwk, xbk, xwv, xbv, xwo, xbo,
                ln_g, ln_b, wq, wk, wv, q_scale, k_scale, wo, gate_w, gate_b, w1, b1, w2, b2, out):
    B = x.shape[0]
    TILES = B * S // P
    GROUPS = B * S // GT
    PER = GT // P
    x_t = x.rearrange("(t b) s d -> (t b s) d", b=2)
    c_t = ctx_in.rearrange("(t b) s d -> (t b s) d", b=2)
    m_t = mask.rearrange("b q k -> q b k")
    out_t = out.rearrange("(t b) s d -> (b s) t d", b=2)

    gates_dram = nc.dram_tensor("gates_dram", (E, B * S), F32).ap()

    def row(v):
        return v.rearrange("(a d) -> a d", a=1)

    def ge(eng, sem, value):
        if not isinstance(value, int) or value > 0:
            eng.wait_ge(sem, value)

    with ExitStack() as stack:
        def sb(name, shape, dt=F32):
            return stack.enter_context(nc.sbuf_tensor(name, shape, dt))

        def psum(name, shape):
            return stack.enter_context(nc.psum_tensor(name, shape, F32))

        def sem(name):
            return stack.enter_context(nc.semaphore(name))

        def split_pair(name, shape):
            hi = sb(name + "_hi", shape, F32R)
            at = (nc.sbuf_base + 31) // 32 * 32
            whole = sb(name + "_whole", shape)
            return hi, nc.alloc_sbuf_tensor_at(name + "_lo", shape, F32R, offset=at), whole

        ps_s = psum("ps_s", [P, 2, 512])
        ps_t = psum("ps_t", [P, 2, 512])
        ps_q = psum("ps_q", [P, 2, 512])
        ps_x = psum("ps_x", [P, 512])
        ps_y = psum("ps_y", [P, 512])

        cst = sb("cst", [P, C_END])
        ident = cst[:, C_ID:C_ID + P]
        causal = cst[:, C_CAUSAL:C_CAUSAL + S]
        par_mask = cst[:, C_PAR:C_PAR + 2]
        pair_mask = cst[:, C_PAIR:C_PAIR + C]
        v_mask = cst[:, C_VM:C_VM + 2 * P].rearrange("p (h f) -> p h f", h=2)
        ident_r = sb("ident_r", [P, P], F32R)
        causal_r = sb("causal_r", [P, C, S], F32R)
        bq_par = sb("bq_par", [P, 2])
        rows = sb("rows", [ROWS, P])
        cols = sb("cols", [P, ROWS])
        qk_scale = sb("qk_scale", [P, C])
        bo_b = sb("bo_b", [P, D])
        g_b = sb("g_b", [P, D])
        b_b = sb("b_b", [P, D])
        gate_bb = sb("gate_bb", [P, E])
        gates_in = sb("gates_in", [P, 2])
        tanh_g = sb("tanh_g", [P, 2])
        tg_bo = sb("tg_bo", [P, D])
        tg_g = sb("tg_g", [P, D])
        tg_b = sb("tg_b", [P, D])
        eps2 = sb("eps2", [P, 4])
        xwT = sb("xwT", [P, 4, D])
        xw = sb("xw", [P, 4, D])
        wqkv_hi, wqkv_lo, wqkv = split_pair("wqkv", [P, 3, INNER])
        wo_s = sb("wo_s", [P, C, D])
        gate_ws = sb("gate_ws", [P, E])
        w1_hi, w1_lo, w1_whole = split_pair("w1", [P, NK, P])
        w2_hi, w2_lo, w2_whole = split_pair("w2", [P, NK, D])
        b2_s = sb("b2_s", [E, D])

        x1_all = sb("x1_all", [P, TILES * D])
        h_hi = sb("h_hi", [P, TILES * P], F32R)
        h_lo = sb("h_lo", [P, TILES * P], F32R)
        gates = sb("gates", [P, TILES * E])
        y_stat = sb("y_stat", [P, PER, 6])
        y_mv = sb("y_mv", [P, PER, 2])
        y_v = sb("y_v", [P, PER])
        y_g = sb("y_g", [P, PER, D])
        y_r = sb("y_r", [P, PER])
        shared = (nc.sbuf_base + 31) // 32 * 32

        x_in = sb("x_in", [P, 2, D])
        c_in = sb("c_in", [P, 2, D])
        m_in = sb("m_in", [P, 2, 2, S], I32)
        x_stat = sb("x_stat", [P, 6])
        x_mv = sb("x_mv", [P, 2])
        x_ln = sb("x_ln", [P, 2])
        x_n = sb("x_n", [P, D])
        xnT = sb("xnT", [P, P])
        ctxT = sb("ctxT", [P, 2, 2, S])
        xq_m = sb("xq_m", [P, 2, 2, S])
        xk_T = sb("xk_T", [P, 2, S])
        xk_m = sb("xk_m", [P, 2, C, S])
        xv_m = sb("xv_m", [P, 2, 2, 2, P])
        x_log = sb("x_log", [P, 2 * C, S])
        x_sh = sb("x_sh", [P, 2 * C, S])
        x_p = x_pn = x_sh
        x_mx = sb("x_mx", [P, 2 * C])
        x_sum = sb("x_sum", [P, 2 * C])
        x_rs = sb("x_rs", [P, 2 * C])
        x_pT = sb("x_pT", [P, 2, 4, 2, S])
        x_aT = sb("x_aT", [P, P])
        x_keep = sb("x_keep", [P, 2, D])
        x1 = sb("x1", [P, 2, D])

        a_stat = sb("a_stat", [P, 6])
        a_mv = sb("a_mv", [P, 2])
        a_ln = sb("a_ln", [P, 2])
        a_n = sb("a_n", [P, D])
        a_hT = sb("a_hT", [P, P])
        a_hi = sb("a_hi", [P, P], F32R)
        a_lo = sb("a_lo", [P, P], F32R)
        a_sq = sb("a_sq", [P, HF, S])
        a_ss = sb("a_ss", [P, 2, HF])
        a_lnss = sb("a_lnss", [P, 2, HF])
        a_r = sb("a_r", [P, 2, HF])
        a_qk = sb("a_qk", [P, 2, HF, S])
        a_qT = sb("a_qT", [P, C, P])
        a_kT = sb("a_kT", [P, C, P])
        a_v = sb("a_v", [P, 2, INNER])
        b_sh = sb("b_sh", [P, 2 * C, S])
        b_p = b_pn = b_sh
        b_mx = sb("b_mx", [P, 2 * C])
        b_sum = sb("b_sum", [P, 2 * C])
        b_rs = sb("b_rs", [P, 2 * C])
        b_pT = sb("b_pT", [P, C, 2, S])
        b_aT = sb("b_aT", [P, C, 2, S])
        b_stat = sb("b_stat", [P, 6])
        b_mv = sb("b_mv", [P, 2])
        b_ln = sb("b_ln", [P, 2])
        b_n = sb("b_n", [P, D])
        b_hT = sb("b_hT", [P, P])
        b_gl = sb("b_gl", [P, E])
        b_gm = sb("b_gm", [P, 1])
        b_ge = sb("b_ge", [P, E])
        b_gs = sb("b_gs", [P, 1])
        b_gr = sb("b_gr", [P, 1])

        RING = 4

        def over(name, shape, dt=F32):
            nonlocal shared
            t = nc.alloc_sbuf_tensor_at(name, shape, dt, offset=shared)
            size = 4
            for n in shape[1:]:
                size *= n
            shared += size
            return t

        hid = over("hid", [P, RING, GT])
        hid_hi = over("hid_hi", [P, RING, GT], F32R)
        hid_lo = over("hid_lo", [P, RING, GT], F32R)
        gT = over("gT", [E, TILES * P])
        gate_rows = over("gate_rows", [P, E, GT])
        e_out = over("e_out", [P, 2, GT])
        y_T = over("y_T", [P, GT])
        y_all = over("y_all", [P, TILES * D])

        tanh_in, xw_in, rows_in, bcast_in = sem("tanh_in"), sem("xw_in"), sem("rows_in"), sem("bcast_in")
        wqkv_in, w1_in, w2_in, small_in = sem("wqkv_in"), sem("w1_in"), sem("w2_in"), sem("small_in")
        inputs_in = [sem(f"inputs_in{p}") for p in range(2)]
        setup_T, setup_cols, setup_xwT, setup_tanh = sem("setup_T"), sem("setup_cols"), sem("setup_xwT"), sem("setup_tanh")
        setup_dve, setup_late = sem("setup_dve"), sem("setup_late")
        wqkv_high, w1_high, w2_high = sem("wqkv_high"), sem("w1_high"), sem("w2_high")
        wqkv_low, w1_low, w2_low = sem("wqkv_low"), sem("w1_low"), sem("w2_low")
        names = ("x_stats x_moments x_log_var x_rstd x_normed x_turned xn_copied ctx_copied x_projected xq_masked "
                 "xk_copied xk_masked xv_masked x_scored x_filled x_masked x_maxed x_shifted x_exped x_summed x_sum_inv "
                 "x_probs x_probs_turned x_probs_copied x_weighted x_attended x_out x1_made x1_kept x_biased "
                 "a_stats a_moments a_log_var a_rstd a_normed a_turned a_scaled a_high a_low q_projected q_squared q_sumsq "
                 "q_log q_rnorm q_normed k_projected k_squared k_sumsq k_log k_rnorm k_normed v_projected v_copied "
                 "q_turned q_copied q_scaled k_turned k_copied "
                 "b_scored b_maxed b_shifted b_exped b_summed b_sum_inv b_probs b_probs_turned b_probs_copied b_weighted "
                 "b_attended b_out b_stats b_moments b_log_var b_rstd b_normed b_turned b_scaled h_high h_low g_projected "
                 "g_biased g_maxed g_exped g_sum_inv g_done ").split()
        s = {n: sem("s_" + n) for n in names}
        hid_ps, hid_done, hid_used = sem("hid_ps"), sem("hid_done"), sem("hid_used")
        hi_act, hi_dve = sem("hi_act"), sem("hi_dve")
        lo_done, out_done, acc_done = sem("lo_done"), sem("out_done"), sem("acc_done")
        gT_ps, gT_done, gT_out = sem("gT_ps"), sem("gT_done"), sem("gT_out")
        gate_row_in = [sem(f"gate_row_in{e}") for e in range(E)]
        y_ps, y_sum, yT_ps, y_stats, y_mvs = sem("y_ps"), sem("y_sum"), sem("yT_ps"), sem("y_stats"), sem("y_mvs")
        y_vs, y_rs = sem("y_vs"), sem("y_rs")
        y_norm, x1_biased, out_ready, stored = sem("y_norm"), sem("x1_biased"), sem("out_ready"), sem("stored")
        passed = sem("passed")

        def hold(eng, sm, value):
            ge(eng, sm, value)
            if not isinstance(value, int):
                eng.sem_inc(passed, 1)

        def done(eng, product, value, alone=False):
            if isinstance(value, int):
                if value > 0:
                    eng.wait_ge(s[product], min(value, TILES))
            elif alone:
                hold(eng, s[product], value)
            else:
                eng.wait_ge(s[product], value)

        def counts(eng, t, p, used):
            n = {k: t + 1 - k if isinstance(t, int) else eng.snap(t + (1 - k)) for k in used}
            return n, [(p + k) % 2 for k in range(LAGS + 1)]

        def run_tiles(eng, body):
            first = (LAGS + 1) // 2 * 2
            for t in range(first):
                body(t, t % 2, t)
            with eng.Fori(first // 2, TILES // 2) as j:
                body(2 * j, 0, None)
                body(2 * j + 1, 1, None)
            for t in range(TILES, TILES + LAGS - 1):
                body(t, t % 2, t)

        def inputs_of(eng, t, k, p):
            if isinstance(t, int):
                return 64 * ((t - k) // 2 + 1)
            return eng.snap(32 * t + (64 - 32 * (p + k)))

        def has(static, k):
            return static is None or 0 <= static - k < TILES

        def hid_bank(k):
            return (ps_s if k % 4 < 2 else ps_t)[:, k % 2, :]

        LAGS = 5
        H = NK // 2
        flat = lambda ap: ap[:, :, :].rearrange("p a b -> p (a b)")
        block = stack.enter_context(nc.Block())

        @block.sync
        def _(sp):
            def load(t, p):
                sp.dma_start(x_in[:, p, :], x_t[bass.ts(t, P)]).then_inc(inputs_in[p], 16)
                sp.dma_start(c_in[:, p, :], c_t[bass.ts(t, P)]).then_inc(inputs_in[p], 16)
                for h in range(2):
                    sp.dma_start(m_in[h * S:(h + 1) * S, p, :, :], m_t[:, bass.ts(t, 2), :]).then_inc(inputs_in[p], 16)

            sp.dma_start(cst[:, :], consts).then_inc(xw_in, 16)
            sp.dma_start(x_in[:, 0, :], x_t[0:P]).then_inc(inputs_in[0], 16)
            sp.dma_start(xw[:, 0, :], xwq).then_inc(xw_in, 16)
            sp.dma_start(xw[:, 2, :], xwv).then_inc(xw_in, 16)
            for h in range(2):
                sp.dma_start(m_in[h * S:(h + 1) * S, 0, :, :], m_t[:, 0:2, :]).then_inc(inputs_in[0], 16)
            for r, v in ((ROW_BQ, xbq), (ROW_BK, xbk), (ROW_BV, xbv), (ROW_G, ln_g), (ROW_B, ln_b)):
                sp.dma_start(rows[r:r + 1, :], row(v)).then_inc(rows_in, 16)
            sp.dma_start(rows[ROW_QS:ROW_QS + C, :], q_scale.rearrange("(c h) a d -> c (h a d)", h=2)).then_inc(rows_in, 16)
            sp.dma_start(rows[ROW_KS:ROW_KS + C, :], k_scale.rearrange("(c h) a d -> c (h a d)", h=2)).then_inc(rows_in, 16)
            sp.dma_start(rows[ROW_B1:ROWS, :], b1.rearrange("e (c f) -> (e c) f", f=P)).then_inc(rows_in, 16)
            for j, w in enumerate((wq, wk, wv)):
                sp.dma_start(wqkv[:, j, :], w).then_inc(wqkv_in, 16)
            load(1, 1)
            sp.dma_start(w1_whole[:, :, :].rearrange("p (e c) f -> p e (c f)", e=E),
                         w1.rearrange("e d f -> d e f")).then_inc(w1_in, 16)
            sp.dma_start(wo_s[:, :, :], wo.rearrange("(c p) d -> p c d", p=P)).then_inc(small_in, 16)
            sp.dma_start(gate_ws[:, :], gate_w).then_inc(small_in, 16)
            sp.dma_start(b2_s[:, :], b2).then_inc(small_in, 16)
            sp.dma_start(w2_whole[:, :, :], w2.rearrange("e (c p) d -> p (e c) d", p=P)).then_inc(w2_in, 16)
            with sp.Fori(0, TILES // 2 - 1) as j:
                i = 2 * j
                for p in range(2):
                    sp.wait_ge(s["x_masked"], i + (p + 1))
                    sp.wait_ge(s["x_biased"], i + (p + 1))
                    load(i + (p + 2), p)
            sp.wait_ge(gT_done, GROUPS)
            sp.dma_start(gates_dram, gT[:, :]).then_inc(gT_out, 16)
            sp.wait_ge(gT_out, 16)

            def gate_row(g, e, first):
                if not first:
                    sp.wait_ge(out_done, g * E + (e + 1 - E))
                sp.dma_start(gate_rows[:, e, :], gates_dram[e, bass.ts(g, GT)].partition_broadcast(P)).then_inc(gate_row_in[e], 16)

            def store(g):
                sp.wait_ge(out_ready, g * PER + PER)
                sp.dma_start(out_t[:, bass.ts(g, PER), :], y_all[:, bass.ts(g, PER * D)]
                             .rearrange("p (t d) -> p t d", d=D)).then_inc(stored, 16)

            for e in range(E):
                gate_row(0, e, True)
            with sp.Fori(1, GROUPS) as g:
                for e in range(E):
                    gate_row(g, e, False)
                    if e == E // 2:
                        store(g - 1)
            store(GROUPS - 1)
            sp.wait_ge(stored, 16 * GROUPS)

        @block.gpsimd
        def _(pool):
            for tile, v in ((bo_b, xbo), (g_b, ln_g), (b_b, ln_b), (gate_bb, gate_b)):
                pool.dma_start(tile[:, :], v.partition_broadcast(P)).then_inc(bcast_in, 16)
            pool.wait_ge(setup_cols, 4)

            def body(t, p, static):
                n, at = counts(pool, t, p, (0, 1, 2, 3))
                if has(static, 1):
                    pool.wait_ge(inputs_in[at[1]], inputs_of(pool, t, 1, at[1]))
                    pool.tensor_tensor(x_keep[:, at[1], :], x_in[:, at[1], :], tg_bo[:, :], ALU.add).then_inc(s["x_biased"], 1)
                    done(pool, "x_maxed", n[1])
                    pool.tensor_tensor(x_sh[:, :, :], x_log[:, :, :], x_mx[:, :].unsqueeze(2).to_broadcast([P, 2 * C, S]),
                                       ALU.subtract).then_inc(s["x_shifted"], 1)
                    done(pool, "x_sum_inv", n[1])
                    pool.tensor_tensor(x_pn[:, :, :], x_p[:, :, :], x_rs[:, :].unsqueeze(2).to_broadcast([P, 2 * C, S]),
                                       ALU.mult).then_inc(s["x_probs"], 1)
                if has(static, 0):
                    done(pool, "xk_copied", n[0])
                    pool.tensor_tensor(xk_m[:, :, :, :], xk_T[:, :, :].unsqueeze(2).to_broadcast([P, 2, C, S]),
                                       pair_mask.unsqueeze(1).unsqueeze(3).to_broadcast([P, 2, C, S]),
                                       ALU.mult).then_inc(s["xk_masked"], 1)
                if has(static, 3):
                    done(pool, "b_sum_inv", n[3])
                    pool.tensor_tensor(b_pn[:, :, :], b_p[:, :, :], b_rs[:, :].unsqueeze(2).to_broadcast([P, 2 * C, S]),
                                       ALU.mult).then_inc(s["b_probs"], 1)
                if has(static, 0):
                    pool.memset(flat(x_log), NEG).then_inc(s["x_filled"], 1)
                if has(static, 2):
                    done(pool, "q_copied", n[2])
                    pool.tensor_tensor(a_qT[:, :, :], a_qT[:, :, :], qk_scale[:, :].unsqueeze(2).to_broadcast([P, C, P]),
                                       ALU.mult).then_inc(s["q_scaled"], 1)

            run_tiles(pool, body)

            pool.wait_ge(s["h_low"], TILES)
            pool.wait_ge(s["g_done"], TILES)
            pool.wait_ge(setup_late, 4)

            def deviation(g):
                ge(pool, y_mvs, g * PER + PER)
                pool.tensor_tensor(y_v[:, :], y_mv[:, :, 1], eps2[:, 0:1].to_broadcast([P, PER]), ALU.add).then_inc(y_vs, 1)
                ge(pool, y_vs, g + 1)
                pool.tensor_tensor(y_r[:, :], y_v[:, :], eps2[:, 3:4].to_broadcast([P, PER]), ALU.pow).then_inc(y_rs, 1)

            def experts(g, first):
                for e in range(E):
                    if e == 0:
                        if not first:
                            hold(pool, yT_ps, g)
                        hold(pool, out_done, g * E + 1)
                        ins = pool.tensor_copy(y_T[:, :], e_out[:, 0, :])
                    else:
                        ge(pool, out_done, g * E + (e + 1))
                        ge(pool, acc_done, g * E + e)
                        ins = pool.tensor_tensor(y_T[:, :], y_T[:, :], e_out[:, e % 2, :], ALU.add)
                    ins.then_inc(acc_done, 1)
                    if e == 1 and not first:
                        deviation(g - 1)
                    if e == 3:
                        x = x1_all[:, bass.ts(g, PER * D)].rearrange("p (t d) -> p t d", d=D)
                        pool.tensor_tensor(x, x, tg_b[:, :].unsqueeze(1).to_broadcast([P, PER, D]), ALU.add).then_inc(x1_biased, 1)

            experts(0, True)
            with pool.Fori(1, GROUPS) as g:
                experts(g, False)
            deviation(GROUPS - 1)

        @block.scalar
        def _(act):
            for j, v in enumerate((g_xattn, g_ffn)):
                act.dma_start(gates_in[:, j:j + 1], v.partition_broadcast(P)).then_inc(tanh_in, 16)
            act.dma_start(c_in[:, 0, :], c_t[0:P]).then_inc(inputs_in[0], 16)
            act.dma_start(xw[:, 1, :], xwk).then_inc(xw_in, 16)
            act.dma_start(xw[:, 3, :], xwo).then_inc(xw_in, 16)
            act.wait_ge(tanh_in, 32)
            act.activation(tanh_g[:, :], gates_in[:, :], ACT.Tanh).then_inc(setup_tanh, 1)
            act.wait_ge(setup_dve, 4)
            act.preload_act_table_set("natural_log_exp_and_others")
            act.wait_ge(setup_T, 1)
            act.copy(flat(xwT), ps_s[:, 0, :]).then_inc(setup_xwT, 1)

            def high(hi, whole, part, loaded, count, made):
                act.wait_ge(loaded, count)
                act.copy(hi[:, part, :], whole[:, part, :]).then_inc(made, 1)

            def body(t, p, static):
                n, at = counts(act, t, p, (0, 1, 2, 3, 4))
                if has(static, 0):
                    done(act, "x_moments", n[0])
                    act.activation(x_ln[:, 0:1], x_mv[:, 1:2], ACT.Ln, bias=eps2[:, 0:1]).then_inc(s["x_log_var"], 1)
                    done(act, "x_log_var", n[0])
                    act.activation(x_ln[:, 1:2], x_ln[:, 0:1], ACT.Exp, scale=-0.5).then_inc(s["x_rstd"], 1)
                if has(static, 1):
                    done(act, "x_shifted", n[1])
                    act.activation(flat(x_p), flat(x_sh), ACT.Exp).then_inc(s["x_exped"], 1)
                if has(static, 0):
                    done(act, "x_turned", n[0])
                    act.copy(ctxT[:, :, :, :], ps_x[:, P:2 * P].rearrange("p (b k) -> p b k", b=2).unsqueeze(2)
                             .to_broadcast([P, 2, 2, S])).then_inc(s["ctx_copied"], 1)
                    act.copy(xnT[:, :], ps_x[:, 0:P]).then_inc(s["xn_copied"], 1)
                if static == 1:
                    high(w1_hi, w1_whole, slice(0, H), w1_in, 16, w1_high)
                if has(static, 4):
                    done(act, "b_probs_turned", n[4])
                    act.copy(b_pT[:, :, :, :].rearrange("p c h q -> p (c h q)"), flat(ps_t)).then_inc(s["b_probs_copied"], 1)
                if has(static, 2):
                    done(act, "q_projected", n[2])
                    act.activation(a_sq[:, :, :].rearrange("p h d -> p (h d)"), flat(ps_q), ACT.Square).then_inc(s["q_squared"], 1)
                if has(static, 3):
                    done(act, "b_shifted", n[3])
                    act.activation(flat(b_p), flat(b_sh), ACT.Exp).then_inc(s["b_exped"], 1)
                if static == 0:
                    act.wait_ge(setup_cols, 3)
                if has(static, 0):
                    done(act, "x_projected", n[0])
                    act.activation(xk_T[:, :, :].rearrange("p b k -> p (b k)"), ps_x[:, P:2 * P], ACT.Identity,
                                   bias=cols[:, ROW_BK:ROW_BK + 1]).then_inc(s["xk_copied"], 1)
                if has(static, 2):
                    done(act, "q_sumsq", n[2])
                    act.activation(a_lnss[:, 0, :], a_ss[:, 0, :], ACT.Ln, bias=eps2[:, 2:3]).then_inc(s["q_log"], 1)
                    done(act, "q_log", n[2])
                    act.activation(a_r[:, 0, :], a_lnss[:, 0, :], ACT.Exp, scale=-0.5).then_inc(s["q_rnorm"], 1)
                if has(static, 0):
                    for h in range(2):
                        last = act.activation(xq_m[:, :, h, :], ps_x[:, 0:P].rearrange("p (b q) -> p b q", b=2), ACT.Identity,
                                              scale=par_mask[:, h:h + 1], bias=bq_par[:, h:h + 1])
                    last.then_inc(s["xq_masked"], 1)
                if static == 0:
                    high(wqkv_hi, wqkv, slice(0, 3), wqkv_in, 48, wqkv_high)
                if static == 1:
                    high(w1_hi, w1_whole, slice(H, NK), w1_in, 16, w1_high)
                if has(static, 4):
                    done(act, "b_weighted", n[4])
                    act.copy(b_aT[:, :, :, :], ps_s[:, :, :].rearrange("p b (c q) -> p c b q", c=C)).then_inc(s["b_attended"], 1)
                if has(static, 1):
                    done(act, "x_probs_turned", n[1])
                    act.copy(x_pT[:, :, :, :, :].rearrange("p b j h q -> p (b j h q)"), flat(ps_t)).then_inc(s["x_probs_copied"], 1)
                if has(static, 2):
                    done(act, "k_projected", n[2])
                    act.activation(a_sq[:, :, :].rearrange("p h d -> p (h d)"), flat(ps_q), ACT.Square).then_inc(s["k_squared"], 1)
                if has(static, 1):
                    done(act, "x_weighted", n[1])
                    act.activation(x_aT[:, :], ps_x[:, 0:P], ACT.Identity, bias=cols[:, ROW_BV:ROW_BV + 1]).then_inc(s["x_attended"], 1)
                if has(static, 2):
                    done(act, "k_sumsq", n[2])
                    act.activation(a_lnss[:, 1, :], a_ss[:, 1, :], ACT.Ln, bias=eps2[:, 2:3]).then_inc(s["k_log"], 1)
                    done(act, "k_log", n[2])
                    act.activation(a_r[:, 1, :], a_lnss[:, 1, :], ACT.Exp, scale=-0.5).then_inc(s["k_rnorm"], 1)
                if has(static, 4):
                    done(act, "b_moments", n[4])
                    act.activation(b_ln[:, 0:1], b_mv[:, 1:2], ACT.Ln, bias=eps2[:, 0:1]).then_inc(s["b_log_var"], 1)
                    done(act, "b_log_var", n[4])
                    act.activation(b_ln[:, 1:2], b_ln[:, 0:1], ACT.Exp, scale=-0.5).then_inc(s["b_rstd"], 1)
                if has(static, 2):
                    done(act, "q_turned", n[2])
                    act.copy(flat(a_qT), flat(ps_t)).then_inc(s["q_copied"], 1)
                if has(static, 4):
                    done(act, "b_turned", n[4])
                    act.activation(b_hT[:, :], ps_y[:, 0:P], ACT.Identity, scale=cols[:, ROW_G:ROW_G + 1],
                                   bias=cols[:, ROW_B:ROW_B + 1]).then_inc(s["b_scaled"], 1)
                if has(static, 1):
                    done(act, "a_moments", n[1])
                    act.activation(a_ln[:, 0:1], a_mv[:, 1:2], ACT.Ln, scale=1.0 + EPS, bias=eps2[:, 1:2]).then_inc(s["a_log_var"], 1)
                    done(act, "a_log_var", n[1])
                    act.activation(a_ln[:, 1:2], a_ln[:, 0:1], ACT.Exp, scale=-0.5).then_inc(s["a_rstd"], 1)
                if static == 1:
                    high(w2_hi, w2_whole, slice(0, NK), w2_in, 16, w2_high)
                if has(static, 2):
                    done(act, "k_turned", n[2])
                    act.copy(flat(a_kT), flat(ps_t)).then_inc(s["k_copied"], 1)
                if has(static, 4):
                    done(act, "b_scaled", n[4], alone=True)
                    act.copy(h_hi[:, bass.ts(t - 4, P)], b_hT[:, :]).then_inc(s["h_high"], 1)
                    done(act, "g_maxed", n[4])
                    act.activation(b_ge[:, :], b_gl[:, :], ACT.Exp, bias=b_gm[:, 0:1], accum_out=b_gs[:, 0:1]).then_inc(s["g_exped"], 1)
                if has(static, 1):
                    done(act, "a_turned", n[1])
                    act.activation(a_hT[:, :], ps_y[:, 0:P], ACT.Identity, scale=cols[:, ROW_G:ROW_G + 1],
                                   bias=cols[:, ROW_B:ROW_B + 1]).then_inc(s["a_scaled"], 1)
                    done(act, "a_scaled", n[1])
                    act.copy(a_hi[:, :], a_hT[:, :]).then_inc(s["a_high"], 1)
                if has(static, 2):
                    done(act, "v_projected", n[2])
                    act.copy(a_v[:, at[2], :], flat(ps_q)).then_inc(s["v_copied"], 1)

            run_tiles(act, body)

            def gelu(g, k):
                ge(act, hid_ps, g * NK + (k + 1))
                if isinstance(g, int) and g == 0:
                    ge(act, lo_done, k + 1 - RING)
                else:
                    act.wait_ge(lo_done, g * NK + (k + 1 - RING))
                act.activation(hid[:, k % RING, :], hid_bank(k), ACT.Gelu_apprx_tanh,
                               bias=cols[:, ROW_B1 + k:ROW_B1 + k + 1]).then_inc(hid_done, 1)
                if k % 2 == 1:
                    if isinstance(g, int) and g == 0:
                        ge(act, hid_used, k + 1 - RING)
                    else:
                        act.wait_ge(hid_used, g * NK + (k + 1 - RING))
                    ge(act, hid_done, g * NK + (k + 1))
                    act.copy(hid_hi[:, k % RING, :], hid[:, k % RING, :]).then_inc(hi_act, 1)

            act.preload_act_table_set("gelu_apprx_tanh_and_others")
            act.wait_ge(s["g_done"], TILES)
            for k in range(NK):
                gelu(0, k)
                for j in range(GROUPS):
                    if k == 1 + j // 2:
                        act.wait_ge(gT_ps, j + 1)
                        act.copy(gT[:, j * GT:(j + 1) * GT], (ps_x, ps_y)[j % 2][0:E, :]).then_inc(gT_done, 1)
            with act.Fori(1, GROUPS) as g:
                for k in range(NK):
                    gelu(g, k)

        @block.vector
        def _(dve):
            for j, e in enumerate((EPS, EPS * EPS, 1e-12, -0.5)):
                dve.memset(eps2[:, j:j + 1], e).then_inc(setup_dve, 1)

            def tables():
                dve.wait_ge(setup_T, 2)
                dve.tensor_copy(cols[:, :], ps_y[:, 0:ROWS]).then_inc(setup_cols, 1)
                dve.wait_ge(setup_cols, 1)
                dve.scalar_tensor_tensor(qk_scale[:, :], cols[:, ROW_QS:ROW_QS + C], 10.0, cols[:, ROW_KS:ROW_KS + C],
                                         ALU.mult, ALU.mult).then_inc(setup_cols, 1)
                dve.tensor_scalar(bq_par[:, :], par_mask, cols[:, ROW_BQ:ROW_BQ + 1], None, ALU.mult).then_inc(setup_cols, 1)
                dve.wait_ge(setup_tanh, 1)
                dve.wait_ge(bcast_in, 64)
                dve.tensor_scalar(tg_bo[:, :], bo_b[:, :], tanh_g[:, 0:1], None, ALU.mult).then_inc(setup_cols, 1)

            def low(lo, whole, hi, part, high_made, count, made):
                dve.wait_ge(high_made, count)
                dve.tensor_tensor(lo[:, part, :], whole[:, part, :], hi[:, part, :].bitcast(F32), ALU.subtract).then_inc(made, 1)

            def body(t, p, static):
                n, at = counts(dve, t, p, (0, 1, 2, 3, 4))
                b_log = ps_s[:, :, :].rearrange("p a (c k) -> p (a c) k", k=S)
                if has(static, 0):
                    dve.wait_ge(inputs_in[at[0]], inputs_of(dve, t, 0, at[0]))
                    dve.bn_stats(x_stat[:, :], x_in[:, at[0], :]).then_inc(s["x_stats"], 1)
                    done(dve, "x_stats", n[0], alone=True)
                    dve.bn_aggr(x_mv[:, :], x_stat[:, :]).then_inc(s["x_moments"], 1)
                    done(dve, "x_rstd", n[0])
                    dve.tensor_scalar(x_n[:, :], x_in[:, at[0], :], x_mv[:, 0:1], x_ln[:, 1:2], ALU.subtract,
                                      ALU.mult).then_inc(s["x_normed"], 1)
                if static == 0:
                    tables()
                if has(static, 2):
                    done(dve, "a_high", n[2])
                    dve.tensor_tensor(a_lo[:, :], a_hT[:, :], a_hi[:, :].bitcast(F32), ALU.subtract).then_inc(s["a_low"], 1)
                if has(static, 3):
                    done(dve, "b_scored", n[3])
                    dve.tensor_reduce(b_mx[:, :], b_log, AX_X, ALU.max).then_inc(s["b_maxed"], 1)
                    done(dve, "b_probs_turned", n[4])
                    done(dve, "b_maxed", n[3])
                    dve.tensor_tensor(b_sh[:, :, :], b_log, b_mx[:, :].unsqueeze(2).to_broadcast([P, 2 * C, S]),
                                      ALU.subtract).then_inc(s["b_shifted"], 1)
                if has(static, 1):
                    done(dve, "x_exped", n[1])
                    dve.tensor_reduce(x_sum[:, :], x_p[:, :, :], AX_X, ALU.add).then_inc(s["x_summed"], 1)
                    done(dve, "x_summed", n[1])
                    dve.reciprocal(x_rs[:, :], x_sum[:, :]).then_inc(s["x_sum_inv"], 1)
                if static == 1:
                    low(wqkv_lo, wqkv, wqkv_hi, slice(0, 2), wqkv_high, 1, wqkv_low)
                if static == 2:
                    low(w2_lo, w2_whole, w2_hi, slice(0, H), w2_high, 1, w2_low)
                if has(static, 2):
                    done(dve, "q_squared", n[2])
                    dve.tensor_reduce(a_ss[:, 0, :], a_sq[:, :, :], AX_X, ALU.add).then_inc(s["q_sumsq"], 1)
                    done(dve, "q_rnorm", n[2])
                    dve.tensor_tensor(a_qk[:, 0, :, :], ps_q[:, :, :].rearrange("p a (h d) -> p (a h) d", d=S),
                                      a_r[:, 0, :].unsqueeze(2).to_broadcast([P, HF, S]), ALU.mult).then_inc(s["q_normed"], 1)
                if has(static, 0):
                    done(dve, "xq_masked", n[0])
                    dve.tensor_tensor(xv_m[:, at[0], :, :, :], ps_x[:, 2 * P:4 * P].rearrange("p (b f) -> p b f", b=2).unsqueeze(2)
                                      .to_broadcast([P, 2, 2, P]), v_mask.unsqueeze(1).to_broadcast([P, 2, 2, P]),
                                      ALU.mult).then_inc(s["xv_masked"], 1)
                if static == 1:
                    low(wqkv_lo, wqkv, wqkv_hi, slice(2, 3), wqkv_high, 1, wqkv_low)
                    low(w1_lo, w1_whole, w1_hi, slice(0, H), w1_high, 1, w1_low)
                    low(w1_lo, w1_whole, w1_hi, slice(H, NK), w1_high, 2, w1_low)
                if static == 2:
                    low(w2_lo, w2_whole, w2_hi, slice(H, NK), w2_high, 1, w2_low)
                if has(static, 3):
                    done(dve, "b_exped", n[3])
                    dve.tensor_reduce(b_sum[:, :], b_p[:, :, :], AX_X, ALU.add).then_inc(s["b_summed"], 1)
                    done(dve, "b_summed", n[3])
                    dve.reciprocal(b_rs[:, :], b_sum[:, :]).then_inc(s["b_sum_inv"], 1)
                if has(static, 2):
                    done(dve, "k_squared", n[2])
                    dve.tensor_reduce(a_ss[:, 1, :], a_sq[:, :, :], AX_X, ALU.add).then_inc(s["k_sumsq"], 1)
                if has(static, 4):
                    done(dve, "b_out", n[4])
                    dve.bn_stats(b_stat[:, :], ps_y[:, 0:D]).then_inc(s["b_stats"], 1)
                if has(static, 1):
                    done(dve, "x_out", n[1])
                    dve.scalar_tensor_tensor(x1[:, at[1], :], ps_x[:, P:2 * P], tanh_g[:, 0:1], x_keep[:, at[1], :], ALU.mult,
                                             ALU.add).then_inc(s["x1_made"], 1)
                if has(static, 4):
                    done(dve, "b_stats", n[4], alone=True)
                    dve.bn_aggr(b_mv[:, :], b_stat[:, :]).then_inc(s["b_moments"], 1)
                if has(static, 2):
                    done(dve, "k_rnorm", n[2])
                    dve.tensor_tensor(a_qk[:, 1, :, :], ps_q[:, :, :].rearrange("p a (h d) -> p (a h) d", d=S),
                                      a_r[:, 1, :].unsqueeze(2).to_broadcast([P, HF, S]), ALU.mult).then_inc(s["k_normed"], 1)
                if has(static, 4):
                    done(dve, "b_rstd", n[4])
                    dve.tensor_scalar(b_n[:, :], ps_y[:, 0:D], b_mv[:, 0:1], b_ln[:, 1:2], ALU.subtract,
                                      ALU.mult).then_inc(s["b_normed"], 1)
                if has(static, 1):
                    done(dve, "x1_made", n[1])
                    dve.bn_stats(a_stat[:, :], x1[:, at[1], :]).then_inc(s["a_stats"], 1)
                    dve.scalar_tensor_tensor(x1_all[:, bass.ts(t - 1, D)], ps_x[:, P:2 * P], tanh_g[:, 0:1], x_keep[:, at[1], :],
                                             ALU.mult, ALU.add).then_inc(s["x1_kept"], 1)
                    done(dve, "a_stats", n[1], alone=True)
                    dve.bn_aggr(a_mv[:, :], a_stat[:, :]).then_inc(s["a_moments"], 1)
                if has(static, 0):
                    done(dve, "x_scored", n[0], alone=True)
                    done(dve, "x_filled", n[0], alone=True)
                    for b in range(2):
                        last = dve.copy_predicated(x_log[:, b * C:(b + 1) * C, :], m_in[:, at[0], b, :].unsqueeze(1)
                                                   .to_broadcast([P, C, S]), ps_s[:, b, :].rearrange("p (c k) -> p c k", k=S))
                    last.then_inc(s["x_masked"], 1)
                if has(static, 4):
                    done(dve, "g_projected", n[4])
                    dve.tensor_tensor(b_gl[:, :], ps_y[:, 0:E], gate_bb[:, :], ALU.add).then_inc(s["g_biased"], 1)
                if has(static, 1):
                    done(dve, "a_rstd", n[1])
                    dve.tensor_scalar(a_n[:, :], x1[:, at[1], :], a_mv[:, 0:1], a_ln[:, 1:2], ALU.subtract,
                                      ALU.mult).then_inc(s["a_normed"], 1)
                if has(static, 4):
                    done(dve, "g_biased", n[4])
                    dve.tensor_reduce(b_gm[:, :], b_gl[:, :], AX_X, ALU.max, negate=True).then_inc(s["g_maxed"], 1)
                if has(static, 0):
                    done(dve, "x_masked", n[0])
                    dve.tensor_reduce(x_mx[:, :], x_log[:, :, :], AX_X, ALU.max).then_inc(s["x_maxed"], 1)
                if has(static, 4):
                    done(dve, "h_high", n[4])
                    dve.tensor_tensor(h_lo[:, bass.ts(t - 4, P)], b_hT[:, :], h_hi[:, bass.ts(t - 4, P)].bitcast(F32),
                                      ALU.subtract).then_inc(s["h_low"], 1)
                    done(dve, "g_exped", n[4])
                    dve.reciprocal(b_gr[:, :], b_gs[:, :]).then_inc(s["g_sum_inv"], 1)
                    done(dve, "g_sum_inv", n[4])
                    dve.tensor_scalar(gates[:, bass.ts(t - 4, E)], b_ge[:, :], b_gr[:, 0:1], None, ALU.mult).then_inc(s["g_done"], 1)
                if static == 0:
                    dve.tensor_scalar(tg_g[:, :], g_b[:, :], tanh_g[:, 1:2], None, ALU.mult).then_inc(setup_late, 1)
                    dve.tensor_scalar(tg_b[:, :], b_b[:, :], tanh_g[:, 1:2], None, ALU.mult).then_inc(setup_late, 1)
                    dve.tensor_copy(ident_r[:, :], ident).then_inc(setup_late, 1)
                    dve.tensor_copy(causal_r[:, :, :], causal.unsqueeze(1).to_broadcast([P, C, S])).then_inc(setup_late, 1)

            run_tiles(dve, body)

            def weigh(g, e, first):
                ge(dve, hid_used, g * NK + (4 * e + 4))
                ge(dve, gate_row_in[e], 16 * g + 16)
                if first:
                    ge(dve, acc_done, e - 1)
                else:
                    ge(dve, acc_done, g * E + (e - 1))
                dve.tensor_tensor(e_out[:, e % 2, :], ps_q[:, e % 2, :], gate_rows[:, e, :], ALU.mult).then_inc(out_done, 1)

            def add_bias(g):
                ge(dve, acc_done, g * E + E)
                ge(dve, y_ps, g + 1)
                dve.tensor_tensor(y_T[:, :], ps_y[:, :], y_T[:, :], ALU.add).then_inc(y_sum, 1)

            def statistics(g, c):
                if c == 0:
                    ge(dve, yT_ps, g + 1)
                dve.bn_stats(y_stat[:, c, :], ps_y[:, c * P:(c + 1) * P]).then_inc(y_stats, 1)
                hold(dve, y_stats, g * PER + (c + 1))
                dve.bn_aggr(y_mv[:, c, :], y_stat[:, c, :]).then_inc(y_mvs, 1)

            def scale(g, c):
                ge(dve, y_mvs, g * PER + (c + 1))
                dve.scalar_tensor_tensor(y_g[:, c, :], ps_y[:, c * P:(c + 1) * P], y_mv[:, c, 0:1], tg_g[:, :],
                                         ALU.subtract, ALU.mult).then_inc(y_norm, 1)

            def finish(g, c):
                if c == 0:
                    ge(dve, x1_biased, g + 1)
                    ge(dve, y_rs, g + 1)
                hold(dve, y_norm, g * PER + (c + 1))
                dve.scalar_tensor_tensor(y_all[:, bass.ts(g * PER + c, D)], y_g[:, c, :], y_r[:, c:c + 1],
                                         x1_all[:, bass.ts(g * PER + c, D)], ALU.mult, ALU.add).then_inc(out_ready, 1)

            def experts(g, first):
                for k in range(NK):
                    ge(dve, hid_done, g * NK + (k + 1))
                    if first:
                        hold(dve, hid_used, k + 1 - RING)
                    else:
                        hold(dve, hid_used, g * NK + (k + 1 - RING))
                    if k % 2 == 0:
                        dve.tensor_copy(hid_hi[:, k % RING, :], hid[:, k % RING, :]).then_inc(hi_dve, 1)
                        ge(dve, hi_dve, g * (NK // 2) + (k // 2 + 1))
                    else:
                        ge(dve, hi_act, g * (NK // 2) + (k // 2 + 1))
                    dve.tensor_tensor(hid_lo[:, k % RING, :], hid[:, k % RING, :], hid_hi[:, k % RING, :].bitcast(F32),
                                      ALU.subtract).then_inc(lo_done, 1)
                    if k == 3 and not first:
                        weigh(g - 1, E - 1, False)
                    if k == 5 and not first:
                        add_bias(g - 1)
                    if 8 <= k < 8 + PER and not first:
                        statistics(g - 1, k - 8)
                    if 12 <= k < 12 + PER and not first:
                        scale(g - 1, k - 12)
                    if 16 <= k < 16 + PER and not first:
                        finish(g - 1, k - 16)
                    if k % 4 == 3 and k > 4:
                        weigh(g, k // 4 - 1, first)

            experts(0, True)
            with dve.Fori(1, GROUPS) as g:
                experts(g, False)
            weigh(GROUPS - 1, E - 1, False)
            add_bias(GROUPS - 1)
            for part in (statistics, scale, finish):
                for c in range(PER):
                    part(GROUPS - 1, c)

        @block.tensor
        def _(pe):
            pe.wait_ge(xw_in, 16 * 5)
            for j in range(4):
                last = pe.transpose(ps_s[:, 0, j * P:(j + 1) * P], xw[:, j, :], ident)
            last.then_inc(setup_T, 1)
            pe.wait_ge(setup_xwT, 1)

            def turn_rows():
                pe.wait_ge(rows_in, 16 * 8)
                pe.transpose(ps_y[:, 0:ROWS], rows[:, :], cst[0:ROWS, C_ID:C_ID + ROWS]).then_inc(setup_T, 1)

            def split_mm(o, l_hi, l_lo, r_hi, r_lo, start=True, stop=True):
                pe.matmul(o, l_hi, r_hi, start=start, stop=False)
                pe.matmul(o, l_hi, r_lo, start=False, stop=False)
                return pe.matmul(o, l_lo, r_hi, start=False, stop=stop)

            def hidden(g, k):
                tok = bass.ts(g, GT)
                split_mm(hid_bank(k), w1_hi[:, k, :], w1_lo[:, k, :], h_hi[:, tok], h_lo[:, tok]).then_inc(hid_ps, 1)

            def transposes(of):
                for c in range(C):
                    last = pe.transpose(ps_t[:, c // 4, (c % 4) * P:(c % 4 + 1) * P], of(c), ident)
                return last

            def project(j):
                for k in range(2):
                    w = slice(k * 512, (k + 1) * 512)
                    last = split_mm(ps_q[:, k, :], a_hi[:, :], a_lo[:, :], wqkv_hi[:, j, w], wqkv_lo[:, j, w])
                return last

            def body(t, p, static):
                n, at = counts(pe, t, p, (0, 1, 2, 3, 4))
                if has(static, 0):
                    done(pe, "x_normed", n[0])
                    pe.transpose(ps_x[:, 0:P], x_n[:, :], ident)
                    pe.transpose(ps_x[:, P:2 * P], c_in[:, at[0], :], ident).then_inc(s["x_turned"], 1)
                if static == 0:
                    turn_rows()
                if has(static, 2):
                    if static == 2:
                        pe.wait_ge(wqkv_low, 2)
                    done(pe, "v_copied", n[3])
                    done(pe, "a_low", n[2])
                    project(0).then_inc(s["q_projected"], 1)
                if has(static, 0):
                    done(pe, "xn_copied", n[0])
                    pe.matmul(ps_x[:, 0:P], xwT[:, 0, :], xnT[:, :], start=True, stop=True)
                    pe.matmul(ps_x[:, P:2 * P], xwT[:, 1, :], ctxT[:, :, 0, :], start=True, stop=True)
                    for b in range(2):
                        last = pe.matmul(ps_x[:, (2 + b) * P:(3 + b) * P], ctxT[:, b, :, :].rearrange("p a k -> p (a k)"),
                                         xwT[:, 2, :], start=True, stop=True)
                    last.then_inc(s["x_projected"], 1)
                if has(static, 4):
                    done(pe, "b_shifted", n[3], alone=True)
                    done(pe, "b_probs_copied", n[4], alone=True)
                    for c in range(C):
                        for h in range(2):
                            for b in range(2):
                                last = pe.matmul(ps_s[h * S:(h + 1) * S, b, c * S:(c + 1) * S],
                                                 a_v[b * S:(b + 1) * S, at[4], (2 * c + h) * S:(2 * c + h + 1) * S],
                                                 b_pT[b * S:(b + 1) * S, c, h, :], start=True, stop=True)
                    last.then_inc(s["b_weighted"], 1)
                if has(static, 1):
                    done(pe, "x_probs", n[1])
                    transposes(lambda c: x_pn[:, 2 * c:2 * c + 2, :].rearrange("p c k -> p (c k)")).then_inc(s["x_probs_turned"], 1)
                if has(static, 2):
                    done(pe, "q_normed", n[2])
                    project(1).then_inc(s["k_projected"], 1)
                if has(static, 1):
                    done(pe, "xv_masked", n[0])
                    done(pe, "x_probs_copied", n[1])
                    for b in range(2):
                        for j in range(4):
                            for h in range(2):
                                last = pe.matmul(ps_x[32 * j:32 * (j + 1), b * S:(b + 1) * S],
                                                 xv_m[:, at[1], b, h, 32 * j:32 * (j + 1)], x_pT[:, b, j, h, :],
                                                 start=(h == 0), stop=(h == 1))
                    last.then_inc(s["x_weighted"], 1)
                if has(static, 4):
                    if static == 4:
                        pe.wait_ge(small_in, 48)
                    done(pe, "b_attended", n[4])
                    for c in range(C):
                        last = pe.matmul(ps_y[:, 0:D], b_aT[:, c, :, :].rearrange("p b q -> p (b q)"), wo_s[:, c, :],
                                         start=(c == 0), stop=(c == C - 1))
                    last.then_inc(s["b_out"], 1)
                if static == TILES + LAGS - 2:
                    pe.wait_ge(w1_low, 2)
                    hidden(0, 0)
                if has(static, 1):
                    done(pe, "x_attended", n[1])
                    pe.matmul(ps_x[:, P:2 * P], x_aT[:, :], xwT[:, 3, :], start=True, stop=True).then_inc(s["x_out"], 1)
                if has(static, 2):
                    transposes(lambda c: a_qk[:, 0, 2 * c:2 * c + 2, :].rearrange("p h d -> p (h d)")).then_inc(s["q_turned"], 1)
                if has(static, 0):
                    done(pe, "xk_masked", n[0])
                    done(pe, "xq_masked", n[0])
                    for b in range(2):
                        last = pe.matmul(ps_s[:, b, :], xq_m[:, b, :, :].rearrange("p h q -> p (h q)"),
                                         xk_m[:, b, :, :].rearrange("p c k -> p (c k)"), start=True, stop=True)
                    last.then_inc(s["x_scored"], 1)
                if has(static, 4):
                    done(pe, "b_normed", n[4])
                    pe.transpose(ps_y[:, 0:P], b_n[:, :], ident).then_inc(s["b_turned"], 1)
                if static == TILES + LAGS - 2:
                    hidden(0, 1)
                if has(static, 2):
                    done(pe, "q_copied", n[2])
                    done(pe, "k_normed", n[2])
                    transposes(lambda c: a_qk[:, 1, 2 * c:2 * c + 2, :].rearrange("p h d -> p (h d)")).then_inc(s["k_turned"], 1)
                if has(static, 4):
                    done(pe, "b_scaled", n[4])
                    pe.matmul(ps_y[:, 0:E], b_hT[:, :], gate_ws[:, :], start=True, stop=True).then_inc(s["g_projected"], 1)
                if has(static, 2):
                    project(2).then_inc(s["v_projected"], 1)
                if has(static, 1):
                    done(pe, "a_normed", n[1])
                    pe.transpose(ps_y[:, 0:P], a_n[:, :], ident).then_inc(s["a_turned"], 1)
                if has(static, 2):
                    if static == 2:
                        pe.wait_ge(setup_late, 4)
                    done(pe, "q_scaled", n[2])
                    done(pe, "k_copied", n[2])
                    for k in range(2):
                        pe.matmul(ps_s[:, k, :], ident_r[:, :], causal_r[:, :, :].rearrange("p c k -> p (c k)"),
                                  start=True, stop=True)
                    for c in range(C):
                        for b in range(2):
                            for h in range(2):
                                o = ps_s[h * S:(h + 1) * S, c // 4, (c % 4) * P + b * S:(c % 4) * P + (b + 1) * S]
                                last = pe.matmul(o, a_qT[h * S:(h + 1) * S, c, b * S:(b + 1) * S],
                                                 a_kT[h * S:(h + 1) * S, c, b * S:(b + 1) * S], start=False, stop=True,
                                                 skip_group_check=True)
                    last.then_inc(s["b_scored"], 1)
                if has(static, 3):
                    done(pe, "b_probs", n[3])
                    transposes(lambda c: b_pn[:, 2 * c:2 * c + 2, :].rearrange("p b k -> p (b k)")).then_inc(s["b_probs_turned"], 1)

            run_tiles(pe, body)

            LAG = 3

            def second(g, j, first):
                e = j // 4
                if j % 4 == 0:
                    if first:
                        ge(pe, out_done, e - 1)
                    else:
                        ge(pe, out_done, g * E + (e - 1))
                ge(pe, lo_done, g * NK + (j + 1))
                split_mm(ps_q[:, e % 2, :], w2_hi[:, j, :], w2_lo[:, j, :], hid_hi[:, j % RING, :],
                         hid_lo[:, j % RING, :], start=(j % 4 == 0), stop=(j % 4 == 3)).then_inc(hid_used, 1)

            def gated_bias(g):
                pe.matmul(ps_y[:, :], b2_s[:, :], gT[:, bass.ts(g, GT)], start=True, stop=True).then_inc(y_ps, 1)

            def turn_sum(g):
                ge(pe, y_sum, g + 1)
                for c in range(PER):
                    last = pe.transpose(ps_y[:, c * P:(c + 1) * P], y_T[:, c * P:(c + 1) * P], ident)
                last.then_inc(yT_ps, 1)

            def experts(g, first):
                for k in range(NK):
                    if first:
                        ge(pe, hid_done, k + 1 - RING)
                    else:
                        pe.wait_ge(hid_done, g * NK + (k + 1 - RING))
                    if k >= 2 or not first:
                        hidden(g, k)
                    for j in range(GROUPS) if first else ():
                        if k == 2 + j // 2:
                            if j == 0:
                                pe.wait_ge(s["g_done"], TILES)
                            ge(pe, gT_done, j - 1)
                            for c in range(PER):
                                i = j * PER + c
                                last = pe.transpose((ps_x, ps_y)[j % 2][0:E, c * P:(c + 1) * P], gates[:, i * E:(i + 1) * E], ident)
                            last.then_inc(gT_ps, 1)
                    if k >= LAG:
                        second(g, k - LAG, first)
                    elif not first:
                        second(g - 1, NK + k - LAG, False)
                    if k == 5 and first:
                        pe.wait_ge(gT_done, GROUPS)
                    if k == 4 and not first:
                        gated_bias(g - 1)
                    if k == 7 and not first:
                        turn_sum(g - 1)

            pe.wait_ge(w2_low, 2)
            experts(0, True)
            with pe.Fori(1, GROUPS) as g:
                experts(g, False)
            for k in range(LAG):
                second(GROUPS - 1, NK + k - LAG, False)
            gated_bias(GROUPS - 1)
            turn_sum(GROUPS - 1)


_INS = ['x', 'ctx_1024', 'mask_BxSxS2_if1', 'g_xattn', 'g_ffn', 'L0_xattn_Wq', 'L0_xattn_bq', 'L0_xattn_Wk', 'L0_xattn_bk',
        'L0_xattn_Wv', 'L0_xattn_bv', 'L0_xattn_Wo', 'L0_xattn_bo', 'L0_ffn_ln_g', 'L0_ffn_ln_b', 'L0_ffn_Wq', 'L0_ffn_Wk',
        'L0_ffn_Wv', 'L0_ffn_q_scale', 'L0_ffn_k_scale', 'L0_ffn_Wo', 'L0_ffn_gate_w', 'L0_ffn_gate_b', 'L0_ffn_w1',
        'L0_ffn_b1', 'L0_ffn_w2', 'L0_ffn_b2']


def _constants(np):
    t = np.zeros((P, C_END), np.float32)
    i = np.arange(P)
    t[i, C_ID + i] = 1.0
    t[:, C_CAUSAL:C_CAUSAL + S] = np.where(np.arange(S)[None, :] <= (i % S)[:, None], 0.0, NEVER)
    head = i // (D // HX)
    for h in range(2):
        t[:, C_PAR + h] = (head % 2 == h) / np.sqrt(np.float32(D // HX))
        t[:, C_VM + h * P:C_VM + (h + 1) * P] = (head % 2 == h)[None, :] & ((head // 2 % 2)[None, :] == (i // S)[:, None])
    for c in range(C):
        t[:, C_PAIR + c] = head // 2 == c
    return t


def kernel(**inputs):
    import numpy as _np
    import concourse.bacc as _bacc
    from concourse import mybir as _mybir
    from concourse.bass_utils import run_bass_kernel_spmd as _run

    nc = _bacc.Bacc("TRN2", target_bir_lowering=False, num_devices=1)
    arrays = {"in_constants_dram": _constants(_np)}
    args = [nc.dram_tensor("in_constants_dram", (P, C_END), _mybir.dt.float32, kind="ExternalInput").ap()]
    for name in _INS:
        a = _np.ascontiguousarray(inputs[name])
        arrays[f"in_{name}_dram"] = a
        args.append(nc.dram_tensor(f"in_{name}_dram", a.shape, _mybir.dt.from_np(a.dtype), kind="ExternalInput").ap())
    out = nc.dram_tensor("out_0_dram", inputs["x"].shape, _mybir.dt.float32, kind="ExternalOutput").ap()
    gated_block(nc, *args, out)
    r = _run(nc, [arrays], core_ids=[0])
    return r.results[0]["out_0_dram"]
```
